# Optimizing a Trainium2 kernel written in Bass

```python
import numpy as np
import jax
import jax.numpy as jnp

def _softmax(x, axis=-1):
    return jax.nn.softmax(x, axis=axis)

def _gelu(x):
    return jax.nn.gelu(x, approximate=True)

def _silu(x):
    return jax.nn.silu(x)

def _sigmoid(x):
    return jax.nn.sigmoid(x)

def _layernorm(x, axis=-1, eps=1e-05):
    m = jnp.mean(x, axis=axis, keepdims=True)
    v = jnp.var(x, axis=axis, keepdims=True)
    return (x - m) / jnp.sqrt(v + eps)

def _scatter_add(tgt, idx, src, axis=0):
    return tgt.at[idx].add(src)

def _segment_sum(src, seg, n):
    return jax.ops.segment_sum(src, seg, n)
kernel_name = 'mk_seq_preln_d1_jaxref_r2_2a0788'

def setup_inputs(seed: int=0):
    np.random.seed(seed)
    _w = jnp.asarray

    def _L0_attn_setup():
        import jax, jax.numpy as jnp
        import numpy as np
        B, N, D = (2, 4096, 512)
        H, Dh = (16, 64)
        P = H * Dh
        EPS = 1e-06
        DECAY_BIAS_SHIFT = 2.0

        def _elu_plus_one(x):
            return jax.nn.elu(x) + 1.0

        def _ssd_scan(q, k, v, a, eps):
            qT = jnp.moveaxis(q, 2, 0)
            kT = jnp.moveaxis(k, 2, 0)
            vT = jnp.moveaxis(v, 2, 0)
            aT = jnp.moveaxis(a, 2, 0)
            Bb, Hh, _, Dk = q.shape
            Dv = v.shape[-1]
            S0 = jnp.zeros((Bb, Hh, Dk, Dv), q.dtype)
            z0 = jnp.zeros((Bb, Hh, Dk), q.dtype)

            def step(carry, inp):
                S, z = carry
                qt, kt, vt, at = inp
                S = at[..., None, None] * S + kt[..., :, None] * vt[..., None, :]
                z = at[..., None] * z + kt
                num = jnp.einsum('bhk,bhkv->bhv', qt, S)
                den = jnp.einsum('bhk,bhk->bh', qt, z) + eps
                return ((S, z), num / den[..., None])
            _, outT = jax.lax.scan(step, (S0, z0), (qT, kT, vT, aT))
            return jnp.moveaxis(outT, 0, 2)
        key = jax.random.key(seed)
        ks = jax.random.split(key, 7)
        s_in = 1.0 / np.sqrt(D)
        s_out = 1.0 / np.sqrt(P)
        return {'x': jax.random.normal(ks[0], (B, N, D), jnp.float32), 'Wq': jax.random.normal(ks[1], (D, P), jnp.float32) * s_in, 'Wk': jax.random.normal(ks[2], (D, P), jnp.float32) * s_in, 'Wv': jax.random.normal(ks[3], (D, P), jnp.float32) * s_in, 'Wo': jax.random.normal(ks[4], (P, D), jnp.float32) * s_out, 'Wa': jax.random.normal(ks[5], (D, H), jnp.float32) * s_in, 'ba': jnp.zeros((H,), jnp.float32)}
    _L0_attn_in = _L0_attn_setup()

    def _L0_ffn_setup():
        import jax, jax.numpy as jnp
        import numpy as np
        B, S, K, N = (8, 4096, 512, 512)
        key = jax.random.key(seed)
        k1, k2, k3, k4 = jax.random.split(key, 4)
        x = jax.random.normal(k1, (B, S, K), dtype=jnp.float32)
        CB = jnp.clip(jnp.round(jax.random.normal(k2, (N, K), dtype=jnp.float32) * 42.0), -127.0, 127.0)
        SCB = jax.random.uniform(k3, (N,), dtype=jnp.float32, minval=0.5, maxval=2.0)
        bias = jax.random.normal(k4, (N,), dtype=jnp.float32) * 0.02
        return {'x': x, 'CB': CB, 'SCB': SCB, 'bias': bias}
    _L0_ffn_in = _L0_ffn_setup()
    _d = {'L0_attn_x': _L0_attn_in['x'], 'L0_attn_Wq': _L0_attn_in['Wq'], 'L0_attn_Wk': _L0_attn_in['Wk'], 'L0_attn_Wv': _L0_attn_in['Wv'], 'L0_attn_Wo': _L0_attn_in['Wo'], 'L0_attn_Wa': _L0_attn_in['Wa'], 'L0_attn_ba': _L0_attn_in['ba'], 'L0_ffn_CB': _L0_ffn_in['CB'], 'L0_ffn_SCB': _L0_ffn_in['SCB'], 'L0_ffn_bias': _L0_ffn_in['bias']}
    _x0 = _d['L0_attn_x']
    _d['L0_attn_x'] = jax.random.normal(jax.random.fold_in(jax.random.key(seed), 1), (4, 2048, 512), dtype=_x0.dtype)
    del _x0
    return _d

def reference(L0_attn_x, L0_attn_Wq, L0_attn_Wk, L0_attn_Wv, L0_attn_Wo, L0_attn_Wa, L0_attn_ba, L0_ffn_CB, L0_ffn_SCB, L0_ffn_bias):

    def _L0_attn_ref(x, Wq, Wk, Wv, Wo, Wa, ba):
        import jax, jax.numpy as jnp
        import numpy as np
        B, N, D = (2, 4096, 512)
        H, Dh = (16, 64)
        P = H * Dh
        EPS = 1e-06
        DECAY_BIAS_SHIFT = 2.0

        def _elu_plus_one(x):
            return jax.nn.elu(x) + 1.0

        def _ssd_scan(q, k, v, a, eps):
            qT = jnp.moveaxis(q, 2, 0)
            kT = jnp.moveaxis(k, 2, 0)
            vT = jnp.moveaxis(v, 2, 0)
            aT = jnp.moveaxis(a, 2, 0)
            Bb, Hh, _, Dk = q.shape
            Dv = v.shape[-1]
            S0 = jnp.zeros((Bb, Hh, Dk, Dv), q.dtype)
            z0 = jnp.zeros((Bb, Hh, Dk), q.dtype)

            def step(carry, inp):
                S, z = carry
                qt, kt, vt, at = inp
                S = at[..., None, None] * S + kt[..., :, None] * vt[..., None, :]
                z = at[..., None] * z + kt
                num = jnp.einsum('bhk,bhkv->bhv', qt, S)
                den = jnp.einsum('bhk,bhk->bh', qt, z) + eps
                return ((S, z), num / den[..., None])
            _, outT = jax.lax.scan(step, (S0, z0), (qT, kT, vT, aT))
            return jnp.moveaxis(outT, 0, 2)
        b, n, _ = x.shape
        q = (x @ Wq).reshape(b, n, H, Dh).transpose(0, 2, 1, 3)
        k = (x @ Wk).reshape(b, n, H, Dh).transpose(0, 2, 1, 3)
        v = (x @ Wv).reshape(b, n, H, Dh).transpose(0, 2, 1, 3)
        q = _elu_plus_one(q)
        k = _elu_plus_one(k)
        a = jax.nn.sigmoid(x @ Wa + ba + DECAY_BIAS_SHIFT)
        a = a.transpose(0, 2, 1)
        out = _ssd_scan(q, k, v, a, EPS)
        out = out.transpose(0, 2, 1, 3).reshape(b, n, P)
        return out @ Wo

    def _L0_ffn_ref(x, CB, SCB, bias):
        import jax, jax.numpy as jnp
        import numpy as np
        B, S, K, N = (8, 4096, 512, 512)
        out = jnp.einsum('bsk,nk->bsn', x, CB)
        out = out * (SCB * (1.0 / 127.0)) + bias
        return out
    x = L0_attn_x
    x = x + _L0_attn_ref(_layernorm(x, axis=-1), L0_attn_Wq, L0_attn_Wk, L0_attn_Wv, L0_attn_Wo, L0_attn_Wa, L0_attn_ba)
    x = x + _L0_ffn_ref(_layernorm(x, axis=-1), L0_ffn_CB, L0_ffn_SCB, L0_ffn_bias)
    return x

_drawn_inputs = setup_inputs


def setup_inputs(seed=0):
    import zlib

    import numpy as np

    out = dict(_drawn_inputs(seed))
    spreads = {'L0_attn_ba': (0.0, 0.522)}
    factors = {'L0_attn_Wq': 3.791, 'L0_ffn_bias': 30.734}
    for name, (base, spread) in spreads.items():
        noise = np.random.default_rng([zlib.crc32(name.encode()), seed]).standard_normal(out[name].shape)
        drawn = base * np.exp(spread * noise) if base else spread * noise
        out[name] = jnp.asarray(drawn.astype(out[name].dtype))
    for name, factor in factors.items():
        out[name] = (out[name] * factor).astype(out[name].dtype)
    return out
```

```python
import concourse.bass as bass
from concourse import mybir
from contextlib import ExitStack


def gated_linear_attention_block(
    nc: bass.Bass,
    x: bass.AP,
    Wq: bass.AP,
    Wk: bass.AP,
    Wv: bass.AP,
    Wo: bass.AP,
    Wa: bass.AP,
    ba: bass.AP,
    CBT: bass.AP,
    SCB: bass.AP,
    bias: bass.AP,
    out: bass.AP,
):
    fp32 = mybir.dt.float32
    fp32r = mybir.dt.float32r
    ALU = mybir.AluOpType
    ACT = mybir.ActivationFunctionType

    B, N, DM = x.shape
    P = Wq.shape[1]
    H = Wa.shape[1]
    DH = P // H
    E = DH + 1
    C = 128
    NC = B * N // C
    CB_ = N // C
    KT = DM // 128
    PT = P // 128
    U = 512
    NQ = 2 * P // U
    NU = 3 * P // U
    HU = U // DH
    GH = 4
    NG = H // GH
    LN_EPS = 1e-5
    DEN_EPS = 1e-6
    SHIFT = 2.0
    FIRST, LAST = 4, NC - 2

    x_rows = x.rearrange("b n d -> (b n) d")
    out_rows = out.rearrange("b n d -> (b n) d")
    attn_rows = nc.dram_tensor("attn_rows", [NC * C, P], fp32).ap()
    decay_rows = nc.dram_tensor("decay_rows", [2, H * C + H], fp32).ap()

    def slab(u):
        w = (Wq, Wk, Wv)[u * U // P]
        c = u * U % P
        return w[:, c:c + U].rearrange("(k p) n -> p k n", p=128)

    def row(eng, n):
        if isinstance(n, int):
            return n * C
        at = eng.snap(n * C)
        eng.compute_val(at)
        return at

    def exists(n):
        return not isinstance(n, int) or 0 <= n < NC

    def wait(eng, sem, value):
        if value is not None:
            eng.wait_ge(sem, value)

    def counts(eng, i, per, offsets):
        found = {}
        for d in offsets:
            if isinstance(i, int):
                found[d] = per * (i + d + 1) if i + d >= 0 else None
            else:
                found[d] = eng.snap(per * (i + d + 1))
                eng.compute_val(found[d])
        return found

    def steps(eng, step, first, last):
        for i in range(first, FIRST):
            step(i, i % 2)
        with eng.Fori(FIRST // 2, LAST // 2) as r:
            for b in range(2):
                step(2 * r + b, b)
        for i in range(LAST, last):
            step(i, i % 2)

    both = ExitStack()
    w_hi = both.enter_context(nc.sbuf_tensor("w_hi", [128, NU, KT, U], fp32r))
    w_lo = both.enter_context(nc.sbuf_tensor("w_lo", [128, NU, KT, U], fp32r))
    scale = both.enter_context(nc.sbuf_tensor("scale", [128, DM], fp32))
    bias_b = both.enter_context(nc.sbuf_tensor("bias_b", [128, DM], fp32))
    at_rows = [both.enter_context(nc.sbuf_tensor(f"at_rows{b}", [128, P], fp32)) for b in range(2)]
    x_in = [both.enter_context(nc.sbuf_tensor(f"x_in{b}", [128, DM], fp32)) for b in range(2)]
    rows_loaded = both.enter_context(nc.semaphore("rows_loaded"))
    xin_loaded = both.enter_context(nc.semaphore("xin_loaded"))
    attn_stored = both.enter_context(nc.semaphore("attn_stored"))
    wo_hi, wo_lo = (w[:, 0:PT // KT, :, :].rearrange("p u k n -> p (u k) n") for w in (w_hi, w_lo))
    wf_hi, wf_lo = (w[:, PT // KT, :, :] for w in (w_hi, w_lo))

    with ExitStack() as ctx:
        def sb(name, shape, dt=fp32):
            return ctx.enter_context(nc.sbuf_tensor(name, shape, dt))

        def pb(name):
            return ctx.enter_context(nc.psum_tensor(name, [128, 512], fp32))

        def sem(name):
            return ctx.enter_context(nc.semaphore(name))

        wa_raw = sb("wa_raw", [128, KT, H])
        wa_hi = sb("wa_hi", [128, KT, H], fp32r)
        wa_lo = sb("wa_lo", [128, KT, H], fp32r)
        xt = [sb(f"xt{b}", [128, DM]) for b in range(2)]
        stats = sb("stats", [128, 6])
        moments = sb("moments", [128, 2])
        vareps = sb("vareps", [128, 1])
        rstd = sb("rstd", [128, 1])
        minus_half = sb("minus_half", [128, 1])
        xT_hi = sb("xT_hi", [128, KT, C], fp32r)
        xT_lo = sb("xT_lo", [128, KT, C], fp32r)
        relu_t = [sb(f"relu_t{b}", [128, U]) for b in range(2)]
        exp_t = [sb(f"exp_t{b}", [128, U]) for b in range(2)]
        q = sb("q", [128, P])
        k = [sb(f"k{b}", [128, P]) for b in range(2)]
        v1 = [sb(f"v1{b}", [128, H, E]) for b in range(2)]
        vw = sb("vw", [128, H, E])
        qT = [sb(f"qT{b}", [128, PT, C]) for b in range(2)]
        kT = sb("kT", [128, PT, C])
        ident = sb("ident", [128, 128])
        eye4 = sb("eye4", [128, GH, C])
        zeros = sb("zeros", [H, C])
        keep = sb("keep", [H, NC])
        ba_c = sb("ba_c", [H, 1])
        minus_ba = sb("minus_ba", [H, 1])
        exp_z = sb("exp_z", [H, C])
        one_exp = sb("one_exp", [H, C])
        aT = sb("aT", [H, C])
        pT = sb("pT", [H, C])
        p_tok = [sb(f"p_tok{b}", [128, H]) for b in range(2)]
        abc = sb("abc", [128, H * C])
        pc = [sb(f"pc{b}", [128, H]) for b in range(2)]
        D = sb("D", [128, H, C])
        M = sb("M", [128, 2 * GH, C])
        S = sb("S", [128, PT, 2, E])
        num = sb("num", [128, H, E])
        den = sb("den", [128, H])
        rden = sb("rden", [128, H])
        attn = sb("attn", [128, P])

        def pieces(t, n):
            dims = " ".join("abc"[:len(t.shape) - 1])
            flat = t[tuple(slice(None) for _ in t.shape)].rearrange(f"p {dims} -> p ({dims})")
            return [flat[:, U * j:U * j + U] for j in range(n)]

        raw = pieces(D, 4) + pieces(abc, 4) + pieces(M, 2) + pieces(attn, 2) + pieces(num, 2) + pieces(vw, 2) \
            + pieces(k[1], 2) + pieces(qT[1], 2) + pieces(D, 4)
        raw2 = pieces(q, 2) + pieces(k[NC % 2], 2) + pieces(qT[NC % 2], 2) + pieces(relu_t[0], 1) \
            + pieces(relu_t[1], 1) + pieces(exp_t[0], 1) + pieces(exp_t[1], 1) + pieces(xt[0], 1) + pieces(xt[1], 1)

        G = [pb(f"G{b}") for b in range(2)]
        T = [pb(f"T{b}") for b in range(2)]
        SC = [pb(f"SC{b}") for b in range(2)]
        PV = pb("PV")
        IN = pb("IN")
        DELTA = GH * E

        raw_loaded = [sem(f"raw_loaded{u}") for u in range(NU)]
        scale_loaded = sem("scale_loaded")
        scaled = sem("scaled")
        wo_loaded = [sem(f"wo_loaded{u}") for u in range(PT // KT)]
        wf_loaded = sem("wf_loaded")
        wf_scaled = sem("wf_scaled")
        w2_hi_ready = sem("w2_hi_ready")
        small_loaded = sem("small_loaded")
        w_hi_ready = sem("w_hi_ready")
        w_lo_ready = sem("w_lo_ready")
        wa_ready = sem("wa_ready")
        blank = sem("blank")
        consts_ready = sem("consts_ready")
        ba_ready = sem("ba_ready")
        x_loaded = sem("x_loaded")
        stats_ready = sem("stats_ready")
        moments_ready = sem("moments_ready")
        vareps_ready = sem("vareps_ready")
        rstd_ready = sem("rstd_ready")
        xn_ready = sem("xn_ready")
        xnT_ready = sem("xnT_ready")
        xT_hi_ready = sem("xT_hi_ready")
        xT_lo_ready = sem("xT_lo_ready")
        unit_ready = [sem(f"unit_ready{u}") for u in range(NU)]
        exp_ready = [sem(f"exp_ready{u}") for u in range(NQ)]
        qk_ready = [sem(f"qk_ready{u}") for u in range(NQ)]
        qkT_ready = [sem(f"qkT_ready{u}") for u in range(NQ)]
        qkT_copied = [sem(f"qkT_copied{u}") for u in range(NQ)]
        v_ready = [sem(f"v_ready{u}") for u in range(NU - NQ)]
        z_ready = sem("z_ready")
        exp_z_ready = sem("exp_z_ready")
        one_exp_ready = sem("one_exp_ready")
        a_ready = sem("a_ready")
        pT_ready = sem("pT_ready")
        decay_ready = sem("decay_ready")
        decay_stored = sem("decay_stored")
        abc_loaded = sem("abc_loaded")
        p_ready = sem("p_ready")
        p_copied = sem("p_copied")
        D_ready = sem("D_ready")
        vw_ready = sem("vw_ready")
        scores_ready = [sem(f"scores_ready{r}") for r in range(2)]
        M_ready = [sem(f"M_ready{r}") for r in range(2)]
        group_ready = [sem(f"group_ready{g}") for g in range(NG)]
        inter_scaled = [sem(f"inter_scaled{g}") for g in range(NG)]
        group_done = [sem(f"group_done{g}") for g in range(NG)]
        den_ready = sem("den_ready")
        rden_ready = sem("rden_ready")
        attn_ready = sem("attn_ready")

        block = ctx.enter_context(nc.Block())

        def t_bank(parity, use):
            return T[(parity + use) % 2]

        @block.sync
        def _(sp):
            sp.dma_start(wa_raw[:, :, :], Wa.rearrange("(k p) h -> p k h", p=128)).then_inc(small_loaded, 16)
            sp.dma_start(ba_c[:, :], ba.rearrange("(h a) -> h a", a=1)).then_inc(small_loaded, 16)
            sp.dma_start(xt[0][:, :], x_rows[0:C, :]).then_inc(x_loaded, 16)
            for u in range(NU):
                if KT * u + KT > len(raw) - 4:
                    sp.wait_ge(w_lo_ready, KT)
                for kt in range(KT):
                    sp.dma_start(raw[KT * u + kt], slab(u)[:, kt, :]).then_inc(raw_loaded[u], 16)
                if u == 0:
                    sp.wait_ge(x_loaded, 16)
                    sp.dma_start(xt[1][:, :], x_rows[C:2 * C, :]).then_inc(x_loaded, 16)
            for t, of in ((scale, SCB), (bias_b, bias)):
                sp.dma_start(t[:, :], of.rearrange("(a n) -> a n", a=1).broadcast_to([128, DM]))\
                    .then_inc(scale_loaded, 16)
            sp.wait_ge(w_lo_ready, NU * KT)

            def second_phase_loads():
                sp.wait_ge(qkT_ready[1], NC)
                sp.wait_ge(group_ready[NG - 1], NC - 1)
                sp.wait_ge(qk_ready[NQ - 1], NC)
                sp.wait_ge(xnT_ready, NC)
                for kt in range(PT):
                    sp.dma_start(raw2[kt], Wo[128 * kt:128 * kt + 128, :]).then_inc(wo_loaded[kt // KT], 16)
                for kt in range(KT):
                    sp.dma_start(raw2[PT + kt], CBT[128 * kt:128 * kt + 128, :]).then_inc(wf_loaded, 16)
                sp.dma_start(at_rows[0][:, :], attn_rows[0:C, :]).then_inc(rows_loaded, 16)
                sp.dma_start(x_in[0][:, :], x_rows[0:C, :]).then_inc(xin_loaded, 16)

            def step(i, b):
                one = counts(sp, i, 1, (-2, -1, 0, 1))
                x16 = counts(sp, i, 16, (1,))
                d32 = counts(sp, i, 32, (1,))
                here, ahead2 = row(sp, i), row(sp, i + 2)
                if exists(i + 2) and exists(i):
                    wait(sp, x_loaded, x16[1])
                    wait(sp, xnT_ready, one[0])
                    sp.dma_start(xt[b][:, :], x_rows[bass.ds(ahead2, C), :]).then_inc(x_loaded, 16)
                if exists(i + 1):
                    decays = decay_rows[1 - b, :]
                    wait(sp, decay_ready, one[1])
                    sp.dma_start(decays[0:H * C].rearrange("(h c) -> h c", h=H), aT[:, :]).then_inc(decay_stored, 16)
                    sp.dma_start(decays[H * C:H * C + H].rearrange("(h c) -> h c", h=H),
                                 pT[:, C - 1:C]).then_inc(decay_stored, 16)
                    sp.wait_ge(decay_stored, d32[1])
                    wait(sp, D_ready, one[0])
                    sp.dma_start(abc[:, :], decays[0:H * C].rearrange("(a n) -> a n", a=1)
                                 .broadcast_to([128, H * C])).then_inc(abc_loaded, 16)
                    sp.dma_start(pc[1 - b][:, :], decays[H * C:H * C + H].rearrange("(a n) -> a n", a=1)
                                 .broadcast_to([128, H])).then_inc(abc_loaded, 16)
                if isinstance(i, int) and i == NC - 1:
                    second_phase_loads()
                if exists(i):
                    wait(sp, attn_ready, one[0])
                    sp.dma_start(attn_rows[bass.ds(here, C), :], attn[:, :]).then_inc(attn_stored, 16)

            steps(sp, step, -1, NC)

        @block.gpsimd
        def _(pool):
            pool.memset(ident[:, :], 0.0).then_inc(blank, 1)
            pool.memset(eye4[:, :, :], 0.0).then_inc(blank, 1)
            pool.memset(keep[:, :], 1.0).then_inc(blank, 1)
            pool.memset(minus_half[:, :], -0.5)
            pool.memset(zeros[:, :], 0.0)
            pool.memset(S[:, :, :, :], 0.0)
            for b in range(2):
                pool.memset(v1[b][:, :, DH:E], 1.0)
            pool.wait_ge(blank, 3)
            pool.memset(keep[:, 0:NC:CB_], 0.0)
            pool.affine_select(out=ident[:, :], in_=ident[:, :], compare_op=ALU.not_equal, fill=1.0,
                               base=0, pattern=[[-1, 128]], channel_multiplier=1)
            pool.affine_select(out=eye4[:, :, :], in_=eye4[:, :, :], compare_op=ALU.not_equal, fill=1.0,
                               base=0, pattern=[[0, GH], [-1, C]], channel_multiplier=1)\
                .then_inc(consts_ready, 1)

            def inverse_deviation(i, d):
                one = counts(pool, i, 1, (d,))
                pool.wait_ge(vareps_ready, one[d])
                pool.tensor_tensor(rstd[:, :], vareps[:, :], minus_half[:, :], ALU.pow).then_inc(rstd_ready, 1)

            def step(i, b):
                if exists(i + 2):
                    inverse_deviation(i, 2)

            pool.wait_ge(consts_ready, 1)
            inverse_deviation(-1, 1)
            steps(pool, step, -1, NC)

        @block.scalar
        def _(act):
            def x_hi(count, parity):
                act.wait_ge(xnT_ready, count)
                act.activation(xT_hi[:, :, :], t_bank(parity, 1)[:, :].rearrange("p (k c) -> p k c", k=KT),
                               ACT.Copy).then_inc(xT_hi_ready, 1)

            act.wait_ge(small_loaded, 32)
            act.activation(wa_hi[:, :, :], wa_raw[:, :, :], ACT.Copy).then_inc(w_hi_ready, 1)
            x_hi(1, 0)
            for u in range(NU):
                act.wait_ge(raw_loaded[u], 16 * KT)
                for kt in range(KT):
                    act.activation(w_hi[:, u, kt, :], raw[KT * u + kt], ACT.Copy).then_inc(w_hi_ready, 1)

            def second_phase_hi():
                act.wait_ge(unit_ready[NU - 1], NC)
                for kt in range(PT):
                    if kt % KT == 0:
                        act.wait_ge(wo_loaded[kt // KT], 16 * KT)
                    act.activation(wo_hi[:, kt, :], raw2[kt], ACT.Copy).then_inc(w2_hi_ready, 1)
                for kt in range(KT):
                    act.wait_ge(wf_scaled, kt + 1)
                    act.activation(wf_hi[:, kt, :], raw2[PT + kt], ACT.Copy).then_inc(w2_hi_ready, 1)

            def step(i, b):
                one = counts(act, i, 1, (0, 1, 2))
                ahead = exists(i + 1)
                if not ahead:
                    second_phase_hi()
                    return
                o = 1 - b

                def elu_parts(u):
                    act.wait_ge(unit_ready[u], one[1])
                    if u >= 2:
                        act.wait_ge(qk_ready[u - 2], one[1])
                    else:
                        wait(act, qk_ready[u + 2], one[0])
                    act.activation(relu_t[u % 2][:, :], G[u % 2][:, :], ACT.Relu)
                    act.activation(exp_t[u % 2][:, :], G[u % 2][:, :], ACT.Exp).then_inc(exp_ready[u], 1)

                def copy_T(u):
                    to = qT[o] if u < NQ // 2 else kT
                    h = u % (NQ // 2)
                    act.wait_ge(qkT_ready[u], one[1])
                    act.activation(to[:, 4 * h:4 * h + 4, :],
                                   t_bank(o, 1 + u)[:, :].rearrange("p (k c) -> p k c", k=4),
                                   ACT.Copy).then_inc(qkT_copied[u], 1)

                def copy_v(j):
                    act.wait_ge(unit_ready[NQ + j], one[1])
                    act.activation(v1[o][:, HU * j:HU * j + HU, 0:DH],
                                   G[j % 2][:, :].rearrange("p (h d) -> p h d", h=HU),
                                   ACT.Copy).then_inc(v_ready[j], 1)

                elu_parts(0)
                act.wait_ge(z_ready, one[1])
                if isinstance(i, int) and i == -1:
                    act.wait_ge(ba_ready, 1)
                wait(act, one_exp_ready, one[0])
                act.activation(exp_z[:, :], t_bank(o, 0)[0:H, 0:C], ACT.Exp,
                               bias=minus_ba[:, :], scale=-1.0).then_inc(exp_z_ready, 1)
                elu_parts(1)
                elu_parts(2)
                copy_T(0)
                elu_parts(3)
                copy_v(0)
                copy_T(1)
                copy_T(2)
                copy_T(3)
                copy_v(1)
                act.wait_ge(p_ready, one[1])
                act.activation(p_tok[o][:, :], t_bank(o, 5)[:, 0:H], ACT.Copy).then_inc(p_copied, 1)
                if exists(i + 2):
                    x_hi(one[2], b)

            steps(act, step, -1, NC)

        @block.vector
        def _(dve):
            def x_stats(count16):
                dve.wait_ge(x_loaded, count16)
                nc.vector.bn_stats(stats[:, :], xt_now[0][:, :]).then_inc(stats_ready, 1)

            def x_moments(count):
                nc.vector.bn_aggr(moments[:, :], stats[:, :]).then_inc(moments_ready, 1)
                dve.wait_ge(moments_ready, count)
                nc.vector.tensor_scalar(vareps[:, :], moments[:, 1:2], LN_EPS, None, ALU.add)\
                    .then_inc(vareps_ready, 1)

            def x_normal(count):
                dve.wait_ge(rstd_ready, count)
                nc.vector.tensor_scalar(xt_now[0][:, :], xt_now[0][:, :], moments[:, 0:1], rstd[:, :],
                                        ALU.subtract, ALU.mult).then_inc(xn_ready, 1)

            def x_lo(count, parity):
                dve.wait_ge(xT_hi_ready, count)
                nc.vector.tensor_tensor(xT_lo[:, :, :],
                                        t_bank(parity, 1)[:, :].rearrange("p (k c) -> p k c", k=KT),
                                        xT_hi[:, :, :].bitcast(fp32), ALU.subtract).then_inc(xT_lo_ready, 1)

            xt_now = [xt[0]]
            x_stats(16)
            dve.wait_ge(small_loaded, 32)
            dve.wait_ge(stats_ready, 1)
            nc.vector.tensor_scalar(minus_ba[:, :], ba_c[:, :], -1.0, -SHIFT, ALU.mult, ALU.add).then_inc(ba_ready, 1)
            x_moments(1)
            dve.wait_ge(w_hi_ready, 1)
            nc.vector.tensor_tensor(wa_lo[:, :, :], wa_raw[:, :, :], wa_hi[:, :, :].bitcast(fp32),
                                    ALU.subtract).then_inc(wa_ready, 1)
            x_normal(1)
            x_lo(1, 0)
            for n in range(NU * KT):
                u, kt = n // KT, n % KT
                dve.wait_ge(w_hi_ready, n + 2)
                nc.vector.tensor_tensor(w_lo[:, u, kt, :], raw[n], w_hi[:, u, kt, :].bitcast(fp32),
                                        ALU.subtract).then_inc(w_lo_ready, 1)
            dve.wait_ge(scale_loaded, 32)
            nc.vector.tensor_scalar(scale[:, :], scale[:, :], 1.0 / 127.0, None, ALU.mult).then_inc(scaled, 1)

            def second_phase_scale():
                dve.wait_ge(wf_loaded, 16 * KT)
                dve.wait_ge(scaled, 1)
                for kt in range(KT):
                    nc.vector.tensor_tensor(raw2[PT + kt], raw2[PT + kt], scale[:, :], ALU.mult)\
                        .then_inc(wf_scaled, 1)

            def second_phase_lo(first, last):
                for kt in range(first, last):
                    to, hi = (wo_lo[:, kt, :], wo_hi[:, kt, :]) if kt < PT else (wf_lo[:, kt - PT, :], wf_hi[:, kt - PT, :])
                    dve.wait_ge(w2_hi_ready, kt + 1)
                    nc.vector.tensor_tensor(to, raw2[kt], hi.bitcast(fp32), ALU.subtract)
            dve.wait_ge(consts_ready, 1)

            def step(i, b):
                one = counts(dve, i, 1, (-1, 0, 1, 2))
                x16 = counts(dve, i, 16, (2,))
                d32 = counts(dve, i, 32, (0, 1))
                a16 = counts(dve, i, 16, (-1,))
                first = not exists(i)
                ahead = exists(i + 1)
                ahead2 = exists(i + 2)
                o = 1 - b

                def elu(u):
                    to = q if u < NQ // 2 else k[o]
                    c = u * U % P
                    dve.wait_ge(exp_ready[u], one[1])
                    if u < NQ // 2:
                        wait(dve, qkT_ready[u], one[0])
                    nc.vector.scalar_tensor_tensor(to[:, c:c + U], exp_t[u % 2][:, :], 1.0, relu_t[u % 2][:, :],
                                                   ALU.min, ALU.add).then_inc(qk_ready[u], 1)

                def masked(r):
                    dve.wait_ge(scores_ready[r], one[0])
                    for e in range(2):
                        made = nc.vector.tensor_tensor(
                            M[:, e:2 * GH:2, :], SC[e][:, :].rearrange("p (h c) -> p h c", h=GH),
                            D[:, 2 * GH * r + e:2 * GH * (r + 1):2, :], ALU.mult)
                    made.then_inc(M_ready[r], 1)

                def group(g):
                    hs = slice(GH * g, GH * g + GH)
                    dve.wait_ge(group_ready[g], one[0])
                    nc.vector.tensor_tensor(num[:, hs, :], IN[:, 0:DELTA].rearrange("p (h e) -> p h e", h=GH),
                                            p_tok[b][:, hs].rearrange("p (h a) -> p h a", a=1)
                                            .broadcast_to([128, GH, E]), ALU.mult).then_inc(inter_scaled[g], 1)
                    for j in range(GH):
                        h = GH * g + j
                        ps = slice(64 * (h % 2), 64 * (h % 2) + 64)
                        c = DELTA + E * (j // 2)
                        nc.vector.scalar_tensor_tensor(S[ps, h // 2, h % 2, :], S[ps, h // 2, h % 2, :],
                                                       pc[b][ps, h:h + 1], IN[ps, c:c + E], ALU.mult, ALU.add)
                    dve.wait_ge(inter_scaled[g], one[0])
                    nc.vector.tensor_tensor(num[:, hs, :], num[:, hs, :],
                                            PV[:, 0:DELTA].rearrange("p (h e) -> p h e", h=GH),
                                            ALU.add).then_inc(group_done[g], 1)

                def decay_matrix(j):
                    made = nc.vector.tensor_tensor_scan(
                        D[:, GH * j:GH * j + GH, :].rearrange("p h c -> p (h c)"),
                        abc[:, GH * j * C:GH * (j + 1) * C],
                        eye4[:, :, :].rearrange("p h c -> p (h c)"), 0.0, ALU.mult, ALU.add)
                    if j == NG - 1:
                        made.then_inc(D_ready, 1)

                if ahead:
                    elu(0)
                if not first:
                    dve.wait_ge(D_ready, one[0])
                    masked(0)
                if ahead:
                    dve.wait_ge(exp_z_ready, one[1])
                    nc.vector.tensor_scalar(one_exp[:, :], exp_z[:, :], 1.0, None, ALU.add).then_inc(one_exp_ready, 1)
                    wait(dve, decay_stored, d32[0])
                    wait(dve, p_ready, one[0])
                    dve.wait_ge(one_exp_ready, one[1])
                    nc.vector.reciprocal(aT[:, :], one_exp[:, :]).then_inc(a_ready, 1)
                    elu(1)
                    dve.wait_ge(a_ready, one[1])
                    nc.vector.tensor_tensor_scan(pT[:, :], aT[:, :], zeros[:, :], keep[:, bass.ds(i + 1, 1)],
                                                 ALU.mult, ALU.add).then_inc(pT_ready, 1)
                    dve.wait_ge(pT_ready, one[1])
                    nc.vector.memset(aT[:, 0:1], 0.0).then_inc(decay_ready, 1)
                if not first:
                    dve.wait_ge(p_copied, one[0])
                    dve.wait_ge(abc_loaded, d32[0])
                    wait(dve, attn_ready, one[-1])
                    group(0)
                if ahead:
                    elu(2)
                if not first:
                    group(1)
                if ahead2:
                    xt_now[0] = xt[b]
                    x_stats(x16[2])
                    dve.wait_ge(stats_ready, one[2])
                if ahead:
                    elu(3)
                if ahead2:
                    x_moments(one[2])
                if not first:
                    masked(1)
                if ahead2:
                    x_normal(one[2])
                if not ahead:
                    second_phase_lo(0, KT)
                if ahead:
                    dve.wait_ge(abc_loaded, d32[1])
                    wait(dve, M_ready[0], one[0])
                    wait(dve, vw_ready, one[0])
                    decay_matrix(0)
                    decay_matrix(1)
                    wait(dve, M_ready[1], one[0])
                    decay_matrix(2)
                if not first:
                    group(2)
                if ahead:
                    decay_matrix(3)
                if not ahead:
                    second_phase_lo(KT, PT)
                    second_phase_scale()
                if ahead2:
                    x_lo(one[2], b)
                if not first:
                    group(3)
                    dve.wait_ge(group_done[NG - 1], one[0])
                    nc.vector.tensor_scalar(den[:, :], num[:, :, DH], DEN_EPS, None, ALU.add).then_inc(den_ready, 1)
                if ahead:
                    dve.wait_ge(D_ready, one[1])
                    dve.wait_ge(v_ready[0], one[1])
                    dve.wait_ge(v_ready[1], one[1])
                    nc.vector.tensor_tensor(vw[:, :, :], v1[o][:, :, :], D[:, :, C - 1:C].broadcast_to([128, H, E]),
                                            ALU.mult).then_inc(vw_ready, 1)
                if not first:
                    dve.wait_ge(den_ready, one[0])
                    nc.vector.reciprocal(rden[:, :], den[:, :]).then_inc(rden_ready, 1)
                    wait(dve, attn_stored, a16[-1])
                    dve.wait_ge(rden_ready, one[0])
                    nc.vector.tensor_tensor(attn[:, :].rearrange("p (h d) -> p h d", h=H), num[:, :, 0:DH],
                                            rden[:, :].rearrange("p (h a) -> p h a", a=1)
                                            .broadcast_to([128, H, DH]), ALU.mult).then_inc(attn_ready, 1)

            steps(dve, step, -1, NC)
            second_phase_lo(PT, PT + KT)

        @block.tensor
        def _(pe):
            def transpose_x(count, parity):
                pe.wait_ge(xn_ready, count)
                for kt in range(KT):
                    made = nc.tensor.transpose(t_bank(parity, 1)[:, C * kt:C * kt + C],
                                               xt[parity][:, 128 * kt:128 * kt + 128], ident[:, :])
                made.then_inc(xnT_ready, 1)

            pe.wait_ge(consts_ready, 1)
            transpose_x(1, 0)

            def step(i, b):
                one = counts(pe, i, 1, (-1, 0, 1, 2))
                first = not exists(i)
                ahead = exists(i + 1)
                ahead2 = exists(i + 2)
                o = 1 - b

                def unit(u):
                    if isinstance(i, int) and i == -1:
                        pe.wait_ge(w_lo_ready, KT * (u + 1))
                    if u >= 2:
                        pe.wait_ge(exp_ready[u - 2] if u - 2 < NQ else v_ready[u - 2 - NQ], one[1])
                    else:
                        wait(pe, v_ready[u], one[0])
                    for n, (kt, xp, w) in enumerate([(kt, xp, w) for kt in range(KT) for xp, w in
                                                     ((xT_hi, w_hi), (xT_hi, w_lo), (xT_lo, w_hi))]):
                        made = nc.tensor.matmul(G[u % 2][:, :], xp[:, kt, :], w[:, u, kt, :],
                                                start=(n == 0), stop=(n == 3 * KT - 1))
                    made.then_inc(unit_ready[u], 1)

                def gate_logits():
                    wait(pe, p_copied, one[0])
                    for n, (kt, xp, w) in enumerate([(kt, xp, w) for kt in range(KT) for xp, w in
                                                     ((xT_hi, wa_hi), (xT_hi, wa_lo), (xT_lo, wa_hi))]):
                        made = nc.tensor.matmul(t_bank(o, 0)[0:H, 0:C], w[:, kt, :], xp[:, kt, :],
                                                start=(n == 0), stop=(n == 3 * KT - 1))
                    made.then_inc(z_ready, 1)

                def transpose_qk(u):
                    of = q if u < NQ // 2 else k[o]
                    c = u * U % P
                    pe.wait_ge(qk_ready[u], one[1])
                    if u == 1:
                        pe.wait_ge(exp_z_ready, one[1])
                    elif u >= 2:
                        pe.wait_ge(qkT_copied[u - 2], one[1])
                    for j in range(4):
                        made = nc.tensor.transpose(t_bank(o, 1 + u)[:, C * j:C * j + C],
                                                   of[:, c + 128 * j:c + 128 * j + 128], ident[:, :])
                    made.then_inc(qkT_ready[u], 1)

                def products():
                    pe.wait_ge(qkT_copied[2], one[1])
                    pe.wait_ge(decay_ready, one[1])
                    nc.tensor.matmul(t_bank(o, 5)[:, 0:H], pT[:, :], ident[0:H, 0:H],
                                     start=True, stop=True).then_inc(p_ready, 1)

                def scores(r):
                    if r == 0:
                        for u in range(NQ):
                            pe.wait_ge(qkT_copied[u], one[0])
                        wait(pe, M_ready[1], one[-1])
                    else:
                        pe.wait_ge(M_ready[0], one[0])
                    for j in range(2 * GH):
                        pair, e = (2 * GH * r + j) // 2, j % 2
                        ps = slice(64 * e, 64 * e + 64)
                        made = nc.tensor.matmul(SC[e][:, C * (j // 2):C * (j // 2) + C], kT[ps, pair, :],
                                                qT[b][ps, pair, :], start=True, stop=True)
                    made.then_inc(scores_ready[r], 1)

                def group(g):
                    if g == 0:
                        pe.wait_ge(vw_ready, one[0])
                        wait(pe, group_done[NG - 1], one[-1])
                    else:
                        pe.wait_ge(group_done[g - 1], one[0])
                    if g % 2 == 0:
                        pe.wait_ge(M_ready[g // 2], one[0])
                    for j in range(GH):
                        h = GH * g + j
                        nc.tensor.matmul(PV[:, E * j:E * j + E], M[:, h % (2 * GH), :], v1[b][:, h, :],
                                         start=True, stop=True)
                    for j in range(GH // 2):
                        pair = GH // 2 * g + j
                        nc.tensor.matmul(IN[:, 2 * E * j:2 * E * j + 2 * E], qT[b][:, pair, :],
                                         S[:, pair, :, :].rearrange("p a e -> p (a e)"), start=True, stop=True)
                    for j in range(GH):
                        h = GH * g + j
                        c = DELTA + E * (j // 2)
                        made = nc.tensor.matmul(IN[64 * (h % 2):64 * (h % 2) + 64, c:c + E],
                                                k[b][:, DH * h:DH * h + DH], vw[:, h, :], start=True, stop=True)
                    made.then_inc(group_ready[g], 1)

                if ahead:
                    pe.wait_ge(xT_lo_ready, one[1])
                    unit(0)
                if not first:
                    scores(0)
                if ahead:
                    if isinstance(i, int) and i == -1:
                        pe.wait_ge(wa_ready, 1)
                    gate_logits()
                    unit(1)
                if not first:
                    group(0)
                if ahead:
                    unit(2)
                if not first:
                    group(1)
                if ahead:
                    transpose_qk(0)
                    unit(3)
                if not first:
                    scores(1)
                if ahead:
                    unit(4)
                    transpose_qk(1)
                    transpose_qk(2)
                if not first:
                    group(2)
                if ahead:
                    transpose_qk(3)
                    unit(5)
                    products()
                if ahead2:
                    pe.wait_ge(qkT_copied[3], one[1])
                    transpose_x(one[2], b)
                if not first:
                    group(3)

            steps(pe, step, -1, NC)

    with ExitStack() as ctx:
        def sb(name, shape, dt=fp32):
            return ctx.enter_context(nc.sbuf_tensor(name, shape, dt))

        def pb(name):
            return ctx.enter_context(nc.psum_tensor(name, [128, 512], fp32))

        def sem(name):
            return ctx.enter_context(nc.semaphore(name))

        ident2 = sb("ident2", [128, 128])
        minus_half2 = sb("minus_half2", [128, 1])
        oT_hi = sb("oT_hi", [128, PT, C], fp32r)
        oT_lo = sb("oT_lo", [128, PT, C], fp32r)
        x1 = [sb(f"x1{b}", [128, DM]) for b in range(2)]
        x1b = [sb(f"x1b{b}", [128, DM]) for b in range(2)]
        x1n = [sb(f"x1n{b}", [128, DM]) for b in range(2)]
        stats2 = sb("stats2", [128, 6])
        moments2 = sb("moments2", [128, 2])
        vareps2 = sb("vareps2", [128, 1])
        rstd2 = sb("rstd2", [128, 1])
        fT_hi = sb("fT_hi", [128, KT, C], fp32r)
        fT_lo = sb("fT_lo", [128, KT, C], fp32r)
        y = [sb(f"y{b}", [128, DM]) for b in range(2)]

        TO = [pb(f"TO{b}") for b in range(2)]
        TF = pb("TF")
        Y = [pb(f"Y{b}") for b in range(2)]
        F = [pb(f"F{b}") for b in range(2)]

        blank2 = sem("blank2")
        consts2_ready = sem("consts2_ready")
        oT_ready = [sem(f"oT_ready{h}") for h in range(2)]
        oT_hi_ready = [sem(f"oT_hi_ready{h}") for h in range(2)]
        oT_lo_ready = [sem(f"oT_lo_ready{h}") for h in range(2)]
        Y_ready = sem("Y_ready")
        x1_ready = sem("x1_ready")
        stats2_ready = sem("stats2_ready")
        moments2_ready = sem("moments2_ready")
        vareps2_ready = sem("vareps2_ready")
        rstd2_ready = sem("rstd2_ready")
        x1n_ready = sem("x1n_ready")
        fT_ready = sem("fT_ready")
        fT_hi_ready = sem("fT_hi_ready")
        fT_lo_ready = sem("fT_lo_ready")
        F_ready = sem("F_ready")
        y_ready = sem("y_ready")
        y_stored = sem("y_stored")

        block = ctx.enter_context(nc.Block())

        @block.sync
        def _(sp):
            def load(at, b):
                sp.dma_start(at_rows[b][:, :], attn_rows[bass.ds(at, C), :]).then_inc(rows_loaded, 16)
                sp.dma_start(x_in[b][:, :], x_rows[bass.ds(at, C), :]).then_inc(xin_loaded, 16)

            sp.wait_ge(attn_stored, 16 * NC)

            def step(i, b):
                one = counts(sp, i, 1, (-2, -1, 0))
                x16 = counts(sp, i, 16, (0,))
                y16 = counts(sp, i, 16, (-2,))
                before, ahead = row(sp, i - 1), row(sp, i + 1)
                if exists(i + 1):
                    wait(sp, rows_loaded, x16[0])
                    wait(sp, xin_loaded, x16[0])
                    wait(sp, oT_ready[1], one[-1])
                    wait(sp, x1_ready, one[-1])
                    load(ahead, 1 - b)
                if exists(i - 1):
                    wait(sp, y_stored, y16[-2])
                    wait(sp, y_ready, one[-1])
                    sp.dma_start(out_rows[bass.ds(before, C), :], y[1 - b][:, :]).then_inc(y_stored, 16)

            steps(sp, step, 0, NC + 1)
            sp.wait_ge(y_stored, 16 * NC)

        @block.gpsimd
        def _(pool):
            pool.memset(ident2[:, :], 0.0).then_inc(blank2, 1)
            pool.memset(minus_half2[:, :], -0.5)
            pool.wait_ge(blank2, 1)
            pool.affine_select(out=ident2[:, :], in_=ident2[:, :], compare_op=ALU.not_equal, fill=1.0,
                               base=0, pattern=[[-1, 128]], channel_multiplier=1).then_inc(consts2_ready, 1)
            pool.wait_ge(consts2_ready, 1)

            def step(i, b):
                if exists(i):
                    one = counts(pool, i, 1, (0,))
                    pool.wait_ge(vareps2_ready, one[0])
                    pool.tensor_tensor(rstd2[:, :], vareps2[:, :], minus_half2[:, :], ALU.pow)\
                        .then_inc(rstd2_ready, 1)

            steps(pool, step, 0, NC)

        def half(h):
            return slice(PT // 2 * h, PT // 2 * (h + 1))

        def tiles(bank):
            return bank[:, :].rearrange("p (k c) -> p k c", c=C)

        @block.scalar
        def _(act):
            def rows_hi(count, h):
                act.wait_ge(oT_ready[h], count)
                act.activation(oT_hi[:, half(h), :], tiles(TO[h]), ACT.Copy).then_inc(oT_hi_ready[h], 1)

            for h in range(2):
                rows_hi(1, h)

            def step(i, b):
                one = counts(act, i, 1, (-1, 0, 1))
                if exists(i - 1):
                    act.wait_ge(fT_ready, one[-1])
                    act.activation(fT_hi[:, :, :], tiles(TF), ACT.Copy).then_inc(fT_hi_ready, 1)
                if exists(i + 1):
                    for h in range(2):
                        rows_hi(one[1], h)

            steps(act, step, 0, NC + 1)

        @block.vector
        def _(dve):
            def rows_lo(count, h):
                dve.wait_ge(oT_hi_ready[h], count)
                nc.vector.tensor_tensor(oT_lo[:, half(h), :], tiles(TO[h]), oT_hi[:, half(h), :].bitcast(fp32),
                                        ALU.subtract).then_inc(oT_lo_ready[h], 1)

            for h in range(2):
                rows_lo(1, h)

            def step(i, b):
                one = counts(dve, i, 1, (-1, 0, 1))
                x16 = counts(dve, i, 16, (0,))
                y16 = counts(dve, i, 16, (-3,))
                here = exists(i)
                if exists(i - 1):
                    dve.wait_ge(fT_hi_ready, one[-1])
                    nc.vector.tensor_tensor(fT_lo[:, :, :], tiles(TF), fT_hi[:, :, :].bitcast(fp32),
                                            ALU.subtract).then_inc(fT_lo_ready, 1)
                if here:
                    dve.wait_ge(Y_ready, one[0])
                    dve.wait_ge(xin_loaded, x16[0])
                    nc.vector.tensor_tensor(x1[b][:, :], Y[b][:, :], x_in[b][:, :], ALU.add).then_inc(x1_ready, 1)
                    dve.wait_ge(x1_ready, one[0])
                    nc.vector.bn_stats(stats2[:, :], x1[b][:, :]).then_inc(stats2_ready, 1)
                    dve.wait_ge(stats2_ready, one[0])
                    nc.vector.tensor_tensor(x1b[b][:, :], x1[b][:, :], bias_b[:, :], ALU.add)
                    nc.vector.bn_aggr(moments2[:, :], stats2[:, :]).then_inc(moments2_ready, 1)
                    dve.wait_ge(moments2_ready, one[0])
                    nc.vector.tensor_scalar(vareps2[:, :], moments2[:, 1:2], LN_EPS, None, ALU.add)\
                        .then_inc(vareps2_ready, 1)
                if exists(i + 1):
                    for h in range(2):
                        rows_lo(one[1], h)
                if here:
                    dve.wait_ge(rstd2_ready, one[0])
                    nc.vector.tensor_scalar(x1n[b][:, :], x1[b][:, :], moments2[:, 0:1], rstd2[:, :],
                                            ALU.subtract, ALU.mult).then_inc(x1n_ready, 1)
                if exists(i - 1):
                    dve.wait_ge(F_ready, one[-1])
                    if exists(i - 3):
                        wait(dve, y_stored, y16[-3])
                    nc.vector.tensor_tensor(y[1 - b][:, :], F[1 - b][:, :], x1b[1 - b][:, :], ALU.add)\
                        .then_inc(y_ready, 1)

            steps(dve, step, 0, NC + 1)

        @block.tensor
        def _(pe):
            def transpose_rows(count, count16, b):
                pe.wait_ge(rows_loaded, count16)
                for h in range(2):
                    if count is not None:
                        pe.wait_ge(oT_lo_ready[h], count)
                    for j in range(4):
                        c = 128 * (4 * h + j)
                        made = nc.tensor.transpose(TO[h][:, C * j:C * j + C], at_rows[b][:, c:c + 128], ident2[:, :])
                    made.then_inc(oT_ready[h], 1)

            pe.wait_ge(consts2_ready, 1)
            transpose_rows(None, 16, 0)

            def passes(to, parts_T, parts_w, kts, tiles_k):
                hi_T, lo_T = parts_T
                hi_w, lo_w = parts_w
                for kt in kts:
                    for n, (a, w) in enumerate(((hi_T, hi_w), (hi_T, lo_w), (lo_T, hi_w))):
                        made = nc.tensor.matmul(to[:, :], a[:, kt, :], w[:, kt, :], start=(kt == 0 and n == 0),
                                                stop=(kt == tiles_k - 1 and n == 2))
                return made

            def step(i, b):
                one = counts(pe, i, 1, (-2, -1, 0))
                x16 = counts(pe, i, 16, (1,))
                if exists(i):
                    for h in range(2):
                        pe.wait_ge(oT_lo_ready[h], one[0])
                    wait(pe, x1_ready, one[-2])
                    passes(Y[b], (oT_hi, oT_lo), (wo_hi, wo_lo), range(0, PT // 2), PT)
                if exists(i - 1):
                    pe.wait_ge(x1n_ready, one[-1])
                    wait(pe, fT_lo_ready, one[-2])
                    for j in range(KT):
                        made = nc.tensor.transpose(TF[:, C * j:C * j + C], x1n[1 - b][:, 128 * j:128 * j + 128],
                                                   ident2[:, :])
                    made.then_inc(fT_ready, 1)
                if exists(i):
                    passes(Y[b], (oT_hi, oT_lo), (wo_hi, wo_lo), range(PT // 2, PT), PT).then_inc(Y_ready, 1)
                if exists(i + 1):
                    transpose_rows(one[0], x16[1], 1 - b)
                if exists(i - 1):
                    pe.wait_ge(fT_lo_ready, one[-1])
                    if exists(i - 3):
                        pe.wait_ge(y_ready, counts(pe, i, 1, (-3,))[-3])
                    passes(F[1 - b], (fT_hi, fT_lo), (wf_hi, wf_lo), range(KT), KT).then_inc(F_ready, 1)

            steps(pe, step, 0, NC + 1)


def kernel(L0_attn_x, L0_attn_Wq, L0_attn_Wk, L0_attn_Wv, L0_attn_Wo, L0_attn_Wa, L0_attn_ba,
           L0_ffn_CB, L0_ffn_SCB, L0_ffn_bias):
    import numpy as np
    import concourse.bacc as bacc
    from concourse.bass_utils import run_bass_kernel_spmd

    ins = dict(x=L0_attn_x, Wq=L0_attn_Wq, Wk=L0_attn_Wk, Wv=L0_attn_Wv, Wo=L0_attn_Wo, Wa=L0_attn_Wa,
               ba=L0_attn_ba, CBT=np.asarray(L0_ffn_CB).T, SCB=L0_ffn_SCB, bias=L0_ffn_bias)
    nc = bacc.Bacc("TRN2", target_bir_lowering=False, num_devices=1)
    arrays, args = {}, {}
    for name, a in ins.items():
        a = np.ascontiguousarray(a)
        arrays[f"in_{name}"] = a
        args[name] = nc.dram_tensor(f"in_{name}", a.shape, mybir.dt.from_np(a.dtype), kind="ExternalInput").ap()
    shape = arrays["in_x"].shape
    args["out"] = nc.dram_tensor("out_rows", shape, mybir.dt.float32, kind="ExternalOutput").ap()
    gated_linear_attention_block(nc, **args)
    got = run_bass_kernel_spmd(nc, [arrays], core_ids=[0])
    return got.results[0]["out_rows"]
```

```python
import concourse.bass as bass
from concourse import mybir
from contextlib import ExitStack


def gated_linear_attention_block(
    nc: bass.Bass,
    x: bass.AP,
    Wq: bass.AP,
    Wk: bass.AP,
    Wv: bass.AP,
    Wo: bass.AP,
    Wa: bass.AP,
    ba: bass.AP,
    CBT: bass.AP,
    SCB: bass.AP,
    bias: bass.AP,
    out: bass.AP,
):
    fp32 = mybir.dt.float32
    fp32r = mybir.dt.float32r
    ALU = mybir.AluOpType
    ACT = mybir.ActivationFunctionType

    B, N, DM = x.shape
    P = Wq.shape[1]
    H = Wa.shape[1]
    DH = P // H
    E = DH + 1
    C = 128
    NC = B * N // C
    CB_ = N // C
    KT = DM // 128
    PT = P // 128
    U = 512
    NP = P // U
    NU = 3 * NP
    QT = U // (2 * C)
    NQ = PT // QT
    HU = U // DH
    GH = 4
    NG = H // GH
    LN_EPS = 1e-5
    DEN_EPS = 1e-6
    SHIFT = 2.0
    FIRST, LAST = 4, NC - 4

    x_rows = x.rearrange("b n d -> (b n) d")
    out_rows = out.rearrange("b n d -> (b n) d")
    attn_rows = nc.dram_tensor("attn_rows", [NC * C, P], fp32).ap()
    decay_rows = nc.dram_tensor("decay_rows", [2, H * C + H], fp32).ap()

    def slab(u):
        w = (Wq, Wk, Wv)[u * U // P]
        c = u * U % P
        return w[:, c:c + U].rearrange("(k p) n -> p k n", p=128)

    def row(eng, n):
        if isinstance(n, int):
            return n * C
        at = eng.snap(n * C)
        eng.compute_val(at)
        return at

    def exists(n):
        return not isinstance(n, int) or 0 <= n < NC

    def wait(eng, sem, value):
        if value is not None:
            eng.wait_ge(sem, value)

    def counts(eng, i, per, offsets):
        found = {}
        for d in offsets:
            if isinstance(i, int):
                found[d] = per * (i + d + 1) if i + d >= 0 else None
            else:
                found[d] = eng.snap(per * (i + d + 1))
                eng.compute_val(found[d])
        return found

    def steps(eng, step, first, last):
        for i in range(first, FIRST):
            step(i, i // 2, i % 2)
        with eng.Fori(FIRST // 2, LAST // 2) as r:
            for b in range(2):
                step(2 * r + b, r, b)
        for i in range(LAST, last):
            step(i, i // 2, i % 2)

    both = ExitStack()
    w_hi = both.enter_context(nc.sbuf_tensor("w_hi", [128, NU, KT, U], fp32r))
    w_lo = both.enter_context(nc.sbuf_tensor("w_lo", [128, NU, KT, U], fp32r))
    scale = both.enter_context(nc.sbuf_tensor("scale", [128, DM], fp32))
    bias_b = both.enter_context(nc.sbuf_tensor("bias_b", [128, DM], fp32))
    at_rows = [both.enter_context(nc.sbuf_tensor(f"at_rows{b}", [128, P], fp32)) for b in range(2)]
    x_in = [both.enter_context(nc.sbuf_tensor(f"x_in{b}", [128, DM], fp32)) for b in range(2)]
    rows_loaded = both.enter_context(nc.semaphore("rows_loaded"))
    xin_loaded = both.enter_context(nc.semaphore("xin_loaded"))
    attn_stored = both.enter_context(nc.semaphore("attn_stored"))
    wo_hi, wo_lo = (w[:, 0:PT // KT, :, :].rearrange("p u k n -> p (u k) n") for w in (w_hi, w_lo))
    wf_hi, wf_lo = (w[:, PT // KT, :, :] for w in (w_hi, w_lo))

    with ExitStack() as ctx:
        def sb(name, shape, dt=fp32):
            return ctx.enter_context(nc.sbuf_tensor(name, shape, dt))

        def pb(name):
            return ctx.enter_context(nc.psum_tensor(name, [128, 512], fp32))

        def sem(name):
            return ctx.enter_context(nc.semaphore(name))

        wa_raw = sb("wa_raw", [128, KT, H])
        wa_hi = sb("wa_hi", [128, KT, H], fp32r)
        wa_lo = sb("wa_lo", [128, KT, H], fp32r)
        xt = [sb(f"xt{b}", [128, DM]) for b in range(2)]
        stats = sb("stats", [128, 2, 6])
        moments = sb("moments", [128, 2, 2])
        vareps = sb("vareps", [128, 2])
        rstd = sb("rstd", [128, 2])
        minus_half = sb("minus_half", [128, 2])
        xT_hi = sb("xT_hi", [128, KT, 2 * C], fp32r)
        xT_lo = sb("xT_lo", [128, KT, 2 * C], fp32r)
        relu_t = [sb(f"relu_t{b}", [128, U]) for b in range(2)]
        exp_t = [sb(f"exp_t{b}", [128, U]) for b in range(2)]
        k = [sb(f"k{b}", [128, P]) for b in range(2)]
        v1 = [sb(f"v1{b}", [128, H, E]) for b in range(2)]
        vw = sb("vw", [128, H, E])
        qT = sb("qT", [128, PT, 2 * C])
        kT = sb("kT", [128, PT, C])
        ident = sb("ident", [128, 128])
        eye4 = sb("eye4", [128, GH, C])
        zeros = sb("zeros", [H, C])
        keep = sb("keep", [H, NC])
        ba_c = sb("ba_c", [H, 1])
        minus_ba = sb("minus_ba", [H, 1])
        exp_z = sb("exp_z", [H, C])
        one_exp = sb("one_exp", [H, C])
        aT = sb("aT", [H, C])
        pT = sb("pT", [H, C])
        p_tok = [sb(f"p_tok{b}", [128, H]) for b in range(2)]
        abc = sb("abc", [128, H * C])
        pc = [sb(f"pc{b}", [128, H]) for b in range(2)]
        D = sb("D", [128, H, C])
        M = sb("M", [128, 2 * GH, C])
        S = sb("S", [128, PT, 2, E])
        num = sb("num", [128, H, E])
        den = sb("den", [128, H])
        rden = sb("rden", [128, H])
        attn = sb("attn", [128, P])

        def pieces(t, n):
            dims = " ".join("abc"[:len(t.shape) - 1])
            flat = t[tuple(slice(None) for _ in t.shape)].rearrange(f"p {dims} -> p ({dims})")
            return [flat[:, U * j:U * j + U] for j in range(n)]

        order = [NP, NP + 1, 0, 1, 2 * NP, 2 * NP + 1]
        raw = pieces(D, 4) + pieces(abc, 4) + pieces(at_rows[0], 2) + pieces(at_rows[1], 2) + pieces(k[1], 2) \
            + pieces(x_in[0], 1) + pieces(x_in[1], 1) + pieces(M, 2) + pieces(attn, 2) + pieces(num, 2) + pieces(vw, 2)
        raw2 = pieces(k[NC % 2], 2) + pieces(relu_t[0], 1) + pieces(relu_t[1], 1) + pieces(exp_t[0], 1) \
            + pieces(exp_t[1], 1) + pieces(xt[0], 1) + pieces(xt[1], 1) + pieces(abc, 4)

        G = [pb(f"G{b}") for b in range(2)]
        T = [pb(f"T{b}") for b in range(2)]
        SC = [pb(f"SC{b}") for b in range(2)]
        PV = pb("PV")
        IN = pb("IN")
        DELTA = GH * E

        raw_loaded = [sem(f"raw_loaded{u}") for u in range(NU)]
        scale_loaded = sem("scale_loaded")
        scaled = sem("scaled")
        wo_loaded = [sem(f"wo_loaded{u}") for u in range(PT // KT)]
        wf_loaded = sem("wf_loaded")
        wf_scaled = sem("wf_scaled")
        w2_hi_ready = sem("w2_hi_ready")
        small_loaded = sem("small_loaded")
        w_hi_ready = sem("w_hi_ready")
        w_lo_ready = sem("w_lo_ready")
        wa_ready = sem("wa_ready")
        blank = sem("blank")
        consts_ready = sem("consts_ready")
        ba_ready = sem("ba_ready")
        x_loaded = [sem(f"x_loaded{b}") for b in range(2)]
        stats_ready = sem("stats_ready")
        moments_ready = sem("moments_ready")
        vareps_ready = sem("vareps_ready")
        rstd_ready = sem("rstd_ready")
        xn_ready = sem("xn_ready")
        xnT_ready = [sem(f"xnT_ready{b}") for b in range(2)]
        xT_hi_ready = [sem(f"xT_hi_ready{b}") for b in range(2)]
        xT_lo_ready = [sem(f"xT_lo_ready{b}") for b in range(2)]
        k_unit_ready = [sem(f"k_unit_ready{j}") for j in range(NP)]
        q_unit_ready = [sem(f"q_unit_ready{u}") for u in range(NQ)]
        v_unit_ready = [sem(f"v_unit_ready{j}") for j in range(NP)]
        exp_k_ready = [sem(f"exp_k_ready{j}") for j in range(NP)]
        exp_q_ready = [sem(f"exp_q_ready{u}") for u in range(NQ)]
        k_ready = [sem(f"k_ready{j}") for j in range(NP)]
        q_ready = [sem(f"q_ready{u}") for u in range(NQ)]
        kT_ready = [sem(f"kT_ready{j}") for j in range(NP)]
        kT_copied = [sem(f"kT_copied{j}") for j in range(NP)]
        v_ready = [sem(f"v_ready{j}") for j in range(NP)]
        z_ready = sem("z_ready")
        exp_z_ready = sem("exp_z_ready")
        one_exp_ready = sem("one_exp_ready")
        a_ready = sem("a_ready")
        pT_ready = sem("pT_ready")
        decay_ready = sem("decay_ready")
        decay_stored = sem("decay_stored")
        abc_loaded = sem("abc_loaded")
        p_ready = sem("p_ready")
        p_copied = sem("p_copied")
        D_ready = sem("D_ready")
        vw_ready = sem("vw_ready")
        scores_ready = [sem(f"scores_ready{r}") for r in range(2)]
        M_ready = [sem(f"M_ready{r}") for r in range(2)]
        group_ready = [sem(f"group_ready{g}") for g in range(NG)]
        inter_scaled = [sem(f"inter_scaled{g}") for g in range(NG)]
        group_done = [sem(f"group_done{g}") for g in range(NG)]
        den_ready = sem("den_ready")
        rden_ready = sem("rden_ready")
        attn_ready = sem("attn_ready")

        block = ctx.enter_context(nc.Block())

        def z_bank():
            return T[0]

        def kT_bank(j, a_odd):
            return T[j] if a_odd else T[1 - j]

        def p_bank(a_odd):
            return T[0] if a_odd else T[1]

        def xT_bank(s):
            return T[s]

        def tokens(s):
            return slice(C * s, C * s + C)

        def tiles_of(bank):
            return bank[:, :].rearrange("p (k c) -> p k c", c=C)

        @block.sync
        def _(sp):
            sp.dma_start(wa_raw[:, :, :], Wa.rearrange("(k p) h -> p k h", p=128)).then_inc(small_loaded, 16)
            sp.dma_start(ba_c[:, :], ba.rearrange("(h a) -> h a", a=1)).then_inc(small_loaded, 16)
            for s in range(2):
                sp.dma_start(xt[s][:, :], x_rows[C * s:C * s + C, :]).then_inc(x_loaded[s], 16)
            for n, u in enumerate(order):
                for kt in range(KT):
                    sp.dma_start(raw[KT * n + kt], slab(u)[:, kt, :]).then_inc(raw_loaded[n], 16)
            for t, of in ((scale, SCB), (bias_b, bias)):
                sp.dma_start(t[:, :], of.rearrange("(a n) -> a n", a=1).broadcast_to([128, DM]))\
                    .then_inc(scale_loaded, 16)

            def second_phase_loads():
                sp.wait_ge(group_ready[NG - 1], NC - 1)
                sp.wait_ge(q_ready[NQ - 1], NC // 2)
                for j in range(NP):
                    sp.wait_ge(k_ready[j], NC)
                sp.wait_ge(xnT_ready[1], NC // 2)
                sp.wait_ge(D_ready, NC)
                for kt in range(PT):
                    sp.dma_start(raw2[kt], Wo[128 * kt:128 * kt + 128, :]).then_inc(wo_loaded[kt // KT], 16)
                for kt in range(KT):
                    sp.dma_start(raw2[PT + kt], CBT[128 * kt:128 * kt + 128, :]).then_inc(wf_loaded, 16)
                sp.dma_start(at_rows[0][:, :], attn_rows[0:C, :]).then_inc(rows_loaded, 16)
                sp.dma_start(x_in[0][:, :], x_rows[0:C, :]).then_inc(xin_loaded, 16)

            def step(i, pair, b):
                one = counts(sp, i, 1, (-2, -1, 0, 1))
                pairs = counts(sp, pair, 1, (1,))
                d32 = counts(sp, i, 32, (1,))
                here = row(sp, i)
                if b == 1 and exists(i + 3):
                    for s in range(2):
                        later = row(sp, i + 3 + s)
                        wait(sp, xnT_ready[s], pairs[1])
                        sp.dma_start(xt[s][:, :], x_rows[bass.ds(later, C), :]).then_inc(x_loaded[s], 16)
                if exists(i + 1):
                    decays = decay_rows[1 - b, :]
                    wait(sp, decay_ready, one[1])
                    sp.dma_start(decays[0:H * C].rearrange("(h c) -> h c", h=H), aT[:, :]).then_inc(decay_stored, 16)
                    sp.dma_start(decays[H * C:H * C + H].rearrange("(h c) -> h c", h=H),
                                 pT[:, C - 1:C]).then_inc(decay_stored, 16)
                    sp.wait_ge(decay_stored, d32[1])
                    if not exists(i):
                        sp.wait_ge(w_lo_ready, 2 * KT)
                    wait(sp, D_ready, one[0])
                    sp.dma_start(abc[:, :], decays[0:H * C].rearrange("(a n) -> a n", a=1)
                                 .broadcast_to([128, H * C])).then_inc(abc_loaded, 16)
                    sp.dma_start(pc[1 - b][:, :], decays[H * C:H * C + H].rearrange("(a n) -> a n", a=1)
                                 .broadcast_to([128, H])).then_inc(abc_loaded, 16)
                if isinstance(i, int) and i == NC - 1:
                    second_phase_loads()
                if exists(i):
                    wait(sp, attn_ready, one[0])
                    sp.dma_start(attn_rows[bass.ds(here, C), :], attn[:, :]).then_inc(attn_stored, 16)

            steps(sp, step, -1, NC)

        @block.gpsimd
        def _(pool):
            pool.memset(ident[:, :], 0.0).then_inc(blank, 1)
            pool.memset(eye4[:, :, :], 0.0).then_inc(blank, 1)
            pool.memset(keep[:, :], 1.0).then_inc(blank, 1)
            pool.memset(minus_half[:, :], -0.5)
            pool.memset(zeros[:, :], 0.0)
            pool.memset(S[:, :, :, :], 0.0)
            for b in range(2):
                pool.memset(v1[b][:, :, DH:E], 1.0)
            pool.wait_ge(blank, 3)
            pool.memset(keep[:, 0:NC:CB_], 0.0)
            pool.affine_select(out=ident[:, :], in_=ident[:, :], compare_op=ALU.not_equal, fill=1.0,
                               base=0, pattern=[[-1, 128]], channel_multiplier=1)
            pool.affine_select(out=eye4[:, :, :], in_=eye4[:, :, :], compare_op=ALU.not_equal, fill=1.0,
                               base=0, pattern=[[0, GH], [-1, C]], channel_multiplier=1)\
                .then_inc(consts_ready, 1)

            def inverse_deviation(count):
                pool.wait_ge(vareps_ready, count)
                pool.tensor_tensor(rstd[:, :], vareps[:, :], minus_half[:, :], ALU.pow).then_inc(rstd_ready, 1)

            def step(i, pair, b):
                if b == 1 and exists(i + 3):
                    inverse_deviation(counts(pool, pair, 1, (2,))[2])

            pool.wait_ge(consts_ready, 1)
            inverse_deviation(1)
            steps(pool, step, -1, NC)

        @block.scalar
        def _(act):
            def x_hi(s, count):
                act.wait_ge(xnT_ready[s], count)
                act.activation(xT_hi[:, :, tokens(s)], tiles_of(xT_bank(s)), ACT.Copy).then_inc(xT_hi_ready[s], 1)

            def split_hi(n):
                act.wait_ge(raw_loaded[n], 16 * KT)
                for kt in range(KT):
                    act.activation(w_hi[:, order[n], kt, :], raw[KT * n + kt], ACT.Copy).then_inc(w_hi_ready, 1)

            act.wait_ge(small_loaded, 32)
            act.activation(wa_hi[:, :, :], wa_raw[:, :, :], ACT.Copy).then_inc(w_hi_ready, 1)
            for s in range(2):
                x_hi(s, 1)
            split_hi(0)
            split_hi(1)

            def second_phase_hi():
                act.wait_ge(v_unit_ready[NP - 1], NC)
                for kt in range(PT):
                    if kt % KT == 0:
                        act.wait_ge(wo_loaded[kt // KT], 16 * KT)
                    act.activation(wo_hi[:, kt, :], raw2[kt], ACT.Copy).then_inc(w2_hi_ready, 1)
                for kt in range(KT):
                    act.wait_ge(wf_scaled, kt + 1)
                    act.activation(wf_hi[:, kt, :], raw2[PT + kt], ACT.Copy).then_inc(w2_hi_ready, 1)

            def step(i, pair, b):
                one = counts(act, i, 1, (0, 1))
                pairs = counts(act, pair, 1, (0, 1))
                start = not exists(i)
                if not exists(i + 1):
                    second_phase_hi()
                    return
                o = 1 - b

                def elu_parts(j, made, made_count, used, used_count, ready):
                    act.wait_ge(made, made_count)
                    wait(act, used, used_count)
                    act.activation(relu_t[j][:, :], G[j][:, :], ACT.Relu)
                    act.activation(exp_t[j][:, :], G[j][:, :], ACT.Exp).then_inc(ready, 1)

                def k_parts(j):
                    if b == 1:
                        elu_parts(j, k_unit_ready[j], one[1], k_ready[j], one[0], exp_k_ready[j])
                    else:
                        elu_parts(j, k_unit_ready[j], one[1], q_ready[NQ - 2 + j], pairs[0], exp_k_ready[j])

                def q_parts(u):
                    if u < 2:
                        elu_parts(u, q_unit_ready[u], pairs[1], k_ready[u], one[1], exp_q_ready[u])
                    else:
                        elu_parts(u % 2, q_unit_ready[u], pairs[1], q_ready[u - 2], pairs[1], exp_q_ready[u])

                def copy_kT(j):
                    act.wait_ge(kT_ready[j], one[1])
                    act.activation(kT[:, 4 * j:4 * j + 4, :], tiles_of(kT_bank(j, o)), ACT.Copy)\
                        .then_inc(kT_copied[j], 1)

                def copy_v(j):
                    act.wait_ge(v_unit_ready[j], one[1])
                    act.activation(v1[o][:, HU * j:HU * j + HU, 0:DH],
                                   G[j][:, :].rearrange("p (h d) -> p h d", h=HU), ACT.Copy).then_inc(v_ready[j], 1)

                def exp_logits():
                    act.wait_ge(z_ready, one[1])
                    if start:
                        act.wait_ge(ba_ready, 1)
                    wait(act, one_exp_ready, one[0])
                    act.activation(exp_z[:, :], z_bank()[0:H, 0:C], ACT.Exp,
                                   bias=minus_ba[:, :], scale=-1.0).then_inc(exp_z_ready, 1)

                def copy_p():
                    act.wait_ge(p_ready, one[1])
                    act.activation(p_tok[o][:, :], p_bank(o)[:, 0:H], ACT.Copy).then_inc(p_copied, 1)

                k_parts(0)
                exp_logits()
                if start:
                    split_hi(2)
                k_parts(1)
                if b == 1:
                    if start:
                        split_hi(3)
                    q_parts(0)
                    if start:
                        split_hi(4)
                    q_parts(1)
                    if start:
                        split_hi(5)
                    copy_kT(0)
                    q_parts(2)
                    copy_kT(1)
                    copy_p()
                    q_parts(3)
                    copy_v(0)
                    copy_v(1)
                else:
                    copy_v(0)
                    copy_kT(0)
                    copy_kT(1)
                    if exists(i + 2):
                        x_hi(0, pairs[1])
                    copy_v(1)
                    if exists(i + 2):
                        x_hi(1, pairs[1])
                    copy_p()

            steps(act, step, -1, NC)

        @block.vector
        def _(dve):
            def x_stats(count16):
                for s in range(2):
                    dve.wait_ge(x_loaded[s], count16)
                    made = nc.vector.bn_stats(stats[:, s, :], xt[s][:, :])
                made.then_inc(stats_ready, 1)

            def x_moments(count):
                for s in range(2):
                    made = nc.vector.bn_aggr(moments[:, s, :], stats[:, s, :])
                made.then_inc(moments_ready, 1)
                dve.wait_ge(moments_ready, count)
                nc.vector.tensor_scalar(vareps[:, :], moments[:, :, 1], LN_EPS, None, ALU.add)\
                    .then_inc(vareps_ready, 1)

            def x_normal(count):
                dve.wait_ge(rstd_ready, count)
                for s in range(2):
                    made = nc.vector.tensor_scalar(xt[s][:, :], xt[s][:, :], moments[:, s, 0:1], rstd[:, s:s + 1],
                                                   ALU.subtract, ALU.mult)
                made.then_inc(xn_ready, 1)

            def x_lo(s, count):
                dve.wait_ge(xT_hi_ready[s], count)
                nc.vector.tensor_tensor(xT_lo[:, :, tokens(s)], tiles_of(xT_bank(s)),
                                        xT_hi[:, :, tokens(s)].bitcast(fp32), ALU.subtract).then_inc(xT_lo_ready[s], 1)

            def split_lo(n):
                for kt in range(KT):
                    dve.wait_ge(w_hi_ready, KT * n + kt + 2)
                    nc.vector.tensor_tensor(w_lo[:, order[n], kt, :], raw[KT * n + kt],
                                            w_hi[:, order[n], kt, :].bitcast(fp32), ALU.subtract).then_inc(w_lo_ready, 1)

            x_stats(16)
            dve.wait_ge(small_loaded, 32)
            dve.wait_ge(stats_ready, 1)
            nc.vector.tensor_scalar(minus_ba[:, :], ba_c[:, :], -1.0, -SHIFT, ALU.mult, ALU.add).then_inc(ba_ready, 1)
            x_moments(1)
            dve.wait_ge(w_hi_ready, 1)
            nc.vector.tensor_tensor(wa_lo[:, :, :], wa_raw[:, :, :], wa_hi[:, :, :].bitcast(fp32),
                                    ALU.subtract).then_inc(wa_ready, 1)
            x_normal(1)
            for s in range(2):
                x_lo(s, 1)
            split_lo(0)
            split_lo(1)

            def second_phase_scale():
                dve.wait_ge(wf_loaded, 16 * KT)
                dve.wait_ge(scaled, 1)
                for kt in range(KT):
                    nc.vector.tensor_tensor(raw2[PT + kt], raw2[PT + kt], scale[:, :], ALU.mult)\
                        .then_inc(wf_scaled, 1)

            def second_phase_lo(first, last):
                for kt in range(first, last):
                    to, hi = (wo_lo[:, kt, :], wo_hi[:, kt, :]) if kt < PT else (wf_lo[:, kt - PT, :], wf_hi[:, kt - PT, :])
                    dve.wait_ge(w2_hi_ready, kt + 1)
                    nc.vector.tensor_tensor(to, raw2[kt], hi.bitcast(fp32), ALU.subtract)
            dve.wait_ge(consts_ready, 1)

            def step(i, pair, b):
                one = counts(dve, i, 1, (-1, 0, 1))
                pairs = counts(dve, pair, 1, (1, 2))
                p16 = counts(dve, pair, 16, (2,))
                d32 = counts(dve, i, 32, (0, 1))
                a16 = counts(dve, i, 16, (-1,))
                start = not exists(i)
                here = exists(i)
                ahead = exists(i + 1)
                wide = b == 1 and ahead
                normal = b == 1 and exists(i + 3)
                o = 1 - b

                def elu_k(j):
                    dve.wait_ge(exp_k_ready[j], one[1])
                    nc.vector.scalar_tensor_tensor(k[o][:, U * j:U * j + U], exp_t[j][:, :], 1.0, relu_t[j][:, :],
                                                   ALU.min, ALU.add).then_inc(k_ready[j], 1)

                def elu_q(u):
                    dve.wait_ge(exp_q_ready[u], pairs[1])
                    wait(dve, group_ready[u], one[0])
                    nc.vector.scalar_tensor_tensor(qT[:, QT * u:QT * u + QT, :].rearrange("p k c -> p (k c)"),
                                                   exp_t[u % 2][:, :], 1.0, relu_t[u % 2][:, :],
                                                   ALU.min, ALU.add).then_inc(q_ready[u], 1)

                def masked(r):
                    dve.wait_ge(scores_ready[r], one[0])
                    for e in range(2):
                        made = nc.vector.tensor_tensor(
                            M[:, e:2 * GH:2, :], SC[e][:, :].rearrange("p (h c) -> p h c", h=GH),
                            D[:, 2 * GH * r + e:2 * GH * (r + 1):2, :], ALU.mult)
                    made.then_inc(M_ready[r], 1)

                def group(g):
                    hs = slice(GH * g, GH * g + GH)
                    dve.wait_ge(group_ready[g], one[0])
                    nc.vector.tensor_tensor(num[:, hs, :], IN[:, 0:DELTA].rearrange("p (h e) -> p h e", h=GH),
                                            p_tok[b][:, hs].rearrange("p (h a) -> p h a", a=1)
                                            .broadcast_to([128, GH, E]), ALU.mult).then_inc(inter_scaled[g], 1)
                    for j in range(GH):
                        h = GH * g + j
                        ps = slice(64 * (h % 2), 64 * (h % 2) + 64)
                        c = DELTA + E * (j // 2)
                        nc.vector.scalar_tensor_tensor(S[ps, h // 2, h % 2, :], S[ps, h // 2, h % 2, :],
                                                       pc[b][ps, h:h + 1], IN[ps, c:c + E], ALU.mult, ALU.add)
                    dve.wait_ge(inter_scaled[g], one[0])
                    nc.vector.tensor_tensor(num[:, hs, :], num[:, hs, :],
                                            PV[:, 0:DELTA].rearrange("p (h e) -> p h e", h=GH),
                                            ALU.add).then_inc(group_done[g], 1)

                def decay_matrix(j):
                    made = nc.vector.tensor_tensor_scan(
                        D[:, GH * j:GH * j + GH, :].rearrange("p h c -> p (h c)"),
                        abc[:, GH * j * C:GH * (j + 1) * C],
                        eye4[:, :, :].rearrange("p h c -> p (h c)"), 0.0, ALU.mult, ALU.add)
                    if j == NG - 1:
                        made.then_inc(D_ready, 1)

                if ahead:
                    elu_k(0)
                if here:
                    dve.wait_ge(D_ready, one[0])
                    masked(0)
                if ahead:
                    dve.wait_ge(exp_z_ready, one[1])
                    nc.vector.tensor_scalar(one_exp[:, :], exp_z[:, :], 1.0, None, ALU.add).then_inc(one_exp_ready, 1)
                    wait(dve, decay_stored, d32[0])
                    wait(dve, p_ready, one[0])
                    dve.wait_ge(one_exp_ready, one[1])
                    nc.vector.reciprocal(aT[:, :], one_exp[:, :]).then_inc(a_ready, 1)
                    elu_k(1)
                    dve.wait_ge(a_ready, one[1])
                    nc.vector.tensor_tensor_scan(pT[:, :], aT[:, :], zeros[:, :], keep[:, bass.ds(i + 1, 1)],
                                                 ALU.mult, ALU.add).then_inc(pT_ready, 1)
                    dve.wait_ge(pT_ready, one[1])
                    nc.vector.memset(aT[:, 0:1], 0.0).then_inc(decay_ready, 1)
                if here:
                    dve.wait_ge(p_copied, one[0])
                    dve.wait_ge(abc_loaded, d32[0])
                    wait(dve, attn_ready, one[-1])
                    group(0)
                if start:
                    split_lo(2)
                if wide:
                    elu_q(0)
                if normal:
                    x_stats(p16[2])
                if start:
                    split_lo(3)
                if here:
                    group(1)
                if normal:
                    dve.wait_ge(stats_ready, pairs[2])
                if wide:
                    elu_q(1)
                if normal:
                    x_moments(pairs[2])
                if start:
                    split_lo(4)
                    split_lo(5)
                    dve.wait_ge(scale_loaded, 32)
                    nc.vector.tensor_scalar(scale[:, :], scale[:, :], 1.0 / 127.0, None, ALU.mult).then_inc(scaled, 1)
                if here:
                    masked(1)
                if normal:
                    x_normal(pairs[2])
                if b == 0 and exists(i + 2):
                    x_lo(0, pairs[1])
                if not ahead:
                    second_phase_lo(0, KT)
                if ahead:
                    if start:
                        dve.wait_ge(w_lo_ready, NU * KT)
                    dve.wait_ge(abc_loaded, d32[1])
                    wait(dve, M_ready[0], one[0])
                    wait(dve, vw_ready, one[0])
                    decay_matrix(0)
                    decay_matrix(1)
                    wait(dve, M_ready[1], one[0])
                    decay_matrix(2)
                if here:
                    group(2)
                if wide:
                    elu_q(2)
                if ahead:
                    decay_matrix(3)
                if not ahead:
                    second_phase_lo(KT, PT)
                    second_phase_scale()
                if b == 0 and exists(i + 2):
                    x_lo(1, pairs[1])
                if here:
                    group(3)
                if wide:
                    elu_q(3)
                if here:
                    dve.wait_ge(group_done[NG - 1], one[0])
                    nc.vector.tensor_scalar(den[:, :], num[:, :, DH], DEN_EPS, None, ALU.add).then_inc(den_ready, 1)
                    dve.wait_ge(den_ready, one[0])
                    nc.vector.reciprocal(rden[:, :], den[:, :]).then_inc(rden_ready, 1)
                    wait(dve, attn_stored, a16[-1])
                    dve.wait_ge(rden_ready, one[0])
                    nc.vector.tensor_tensor(attn[:, :].rearrange("p (h d) -> p h d", h=H), num[:, :, 0:DH],
                                            rden[:, :].rearrange("p (h a) -> p h a", a=1)
                                            .broadcast_to([128, H, DH]), ALU.mult).then_inc(attn_ready, 1)
                if ahead:
                    dve.wait_ge(D_ready, one[1])
                    for j in range(NP):
                        dve.wait_ge(v_ready[j], one[1])
                    nc.vector.tensor_tensor(vw[:, :, :], v1[o][:, :, :], D[:, :, C - 1:C].broadcast_to([128, H, E]),
                                            ALU.mult).then_inc(vw_ready, 1)

            steps(dve, step, -1, NC)
            second_phase_lo(PT, PT + KT)

        @block.tensor
        def _(pe):
            def transpose_x(s, count):
                pe.wait_ge(xn_ready, count)
                for kt in range(KT):
                    made = nc.tensor.transpose(xT_bank(s)[:, C * kt:C * kt + C],
                                               xt[s][:, 128 * kt:128 * kt + 128], ident[:, :])
                made.then_inc(xnT_ready[s], 1)

            pe.wait_ge(consts_ready, 1)
            for s in range(2):
                transpose_x(s, 1)

            def step(i, pair, b):
                one = counts(pe, i, 1, (-1, 0, 1))
                pairs = counts(pe, pair, 1, (0, 1))
                start = not exists(i)
                here = exists(i)
                ahead = exists(i + 1)
                wide = b == 1 and ahead
                o = 1 - b

                def product(to, passes):
                    for n, (lhs, rhs) in enumerate(passes):
                        made = nc.tensor.matmul(to, lhs, rhs, start=(n == 0), stop=(n == len(passes) - 1))
                    return made

                def unit(j, slab_of, ready):
                    if start:
                        pe.wait_ge(w_lo_ready, KT * (order.index(slab_of) + 1))
                    product(G[j][:, :], [(xp[:, kt, tokens(o)], w[:, slab_of, kt, :]) for kt, xp, w in parts])\
                        .then_inc(ready, 1)

                parts = [(kt, xp, w) for kt in range(KT)
                         for xp, w in ((xT_hi, w_hi), (xT_hi, w_lo), (xT_lo, w_hi))]

                def k_unit(j):
                    wait(pe, v_ready[j], one[0])
                    unit(j, NP + j, k_unit_ready[j])

                def v_unit(j):
                    if wide:
                        pe.wait_ge(exp_q_ready[NQ - 2 + j], pairs[1])
                    else:
                        pe.wait_ge(exp_k_ready[j], one[1])
                    unit(j, 2 * NP + j, v_unit_ready[j])

                def q_unit(u):
                    if start:
                        pe.wait_ge(w_lo_ready, KT * (order.index(u * QT // KT) + 1))
                    if u == 0:
                        for s in range(2):
                            pe.wait_ge(xT_lo_ready[s], pairs[1])
                    if u < 2:
                        pe.wait_ge(exp_k_ready[u], one[1])
                    else:
                        pe.wait_ge(exp_q_ready[u - 2], pairs[1])
                    for j in range(QT):
                        t = QT * u + j
                        c = 128 * t % U
                        made = product(G[u % 2][:, 2 * C * j:2 * C * j + 2 * C],
                                       [(w[:, 128 * t // U, kt, c:c + 128], xp[:, kt, :]) for kt, xp, w in parts])
                    made.then_inc(q_unit_ready[u], 1)

                def gate_logits():
                    if start:
                        pe.wait_ge(wa_ready, 1)
                    wait(pe, p_copied, one[0])
                    product(z_bank()[0:H, 0:C], [((wa_lo if w is w_lo else wa_hi)[:, kt, :], xp[:, kt, tokens(o)])
                                                 for kt, xp, w in parts]).then_inc(z_ready, 1)

                def transpose_k(j):
                    pe.wait_ge(k_ready[j], one[1])
                    if kT_bank(j, o) is z_bank():
                        pe.wait_ge(exp_z_ready, one[1])
                    elif b == 1:
                        pe.wait_ge(xT_lo_ready[1], pairs[1])
                    else:
                        pe.wait_ge(p_copied, one[0])
                    for t in range(4):
                        c = U * j + 128 * t
                        made = nc.tensor.transpose(kT_bank(j, o)[:, C * t:C * t + C], k[o][:, c:c + 128], ident[:, :])
                    made.then_inc(kT_ready[j], 1)

                def products():
                    if b == 1:
                        pe.wait_ge(kT_copied[0], one[1])
                    elif exists(i + 2):
                        pe.wait_ge(xT_lo_ready[0], pairs[1])
                    else:
                        pe.wait_ge(kT_copied[0], one[1])
                    pe.wait_ge(decay_ready, one[1])
                    nc.tensor.matmul(p_bank(o)[:, 0:H], pT[:, :], ident[0:H, 0:H],
                                     start=True, stop=True).then_inc(p_ready, 1)

                def transpose_next(s):
                    if exists(i + 2):
                        pe.wait_ge(kT_copied[s], one[1])
                        transpose_x(s, pairs[1])

                def scores(r):
                    if r == 0:
                        for j in range(NP):
                            pe.wait_ge(kT_copied[j], one[0])
                        for u in range(NQ):
                            pe.wait_ge(q_ready[u], pairs[0])
                        wait(pe, M_ready[1], one[-1])
                    else:
                        pe.wait_ge(M_ready[0], one[0])
                    for j in range(2 * GH):
                        two, e = (2 * GH * r + j) // 2, j % 2
                        ps = slice(64 * e, 64 * e + 64)
                        made = nc.tensor.matmul(SC[e][:, C * (j // 2):C * (j // 2) + C], kT[ps, two, :],
                                                qT[ps, two, tokens(b)], start=True, stop=True)
                    made.then_inc(scores_ready[r], 1)

                def group(g):
                    if g == 0:
                        pe.wait_ge(vw_ready, one[0])
                        wait(pe, group_done[NG - 1], one[-1])
                    else:
                        pe.wait_ge(group_done[g - 1], one[0])
                    if g % 2 == 0:
                        pe.wait_ge(M_ready[g // 2], one[0])
                    for j in range(GH):
                        h = GH * g + j
                        nc.tensor.matmul(PV[:, E * j:E * j + E], M[:, h % (2 * GH), :], v1[b][:, h, :],
                                         start=True, stop=True)
                    for j in range(GH // 2):
                        two = GH // 2 * g + j
                        nc.tensor.matmul(IN[:, 2 * E * j:2 * E * j + 2 * E], qT[:, two, tokens(b)],
                                         S[:, two, :, :].rearrange("p a e -> p (a e)"), start=True, stop=True)
                    for j in range(GH):
                        h = GH * g + j
                        c = DELTA + E * (j // 2)
                        made = nc.tensor.matmul(IN[64 * (h % 2):64 * (h % 2) + 64, c:c + E],
                                                k[b][:, DH * h:DH * h + DH], vw[:, h, :], start=True, stop=True)
                    made.then_inc(group_ready[g], 1)

                if ahead:
                    pe.wait_ge(xT_lo_ready[o], pairs[1] if b == 1 else pairs[0])
                    k_unit(0)
                if here:
                    scores(0)
                if ahead:
                    gate_logits()
                    k_unit(1)
                if here:
                    group(0)
                if wide:
                    q_unit(0)
                elif ahead:
                    v_unit(0)
                if here:
                    group(1)
                if wide:
                    q_unit(1)
                if here:
                    scores(1)
                if wide:
                    transpose_k(0)
                    q_unit(2)
                elif ahead:
                    transpose_k(0)
                    transpose_k(1)
                    transpose_next(0)
                if here:
                    group(2)
                if wide:
                    transpose_k(1)
                    products()
                    q_unit(3)
                    if here:
                        group(3)
                    v_unit(0)
                    v_unit(1)
                else:
                    if ahead:
                        v_unit(1)
                        transpose_next(1)
                        products()
                    group(3)

            steps(pe, step, -1, NC)

    with ExitStack() as ctx:
        def sb(name, shape, dt=fp32):
            return ctx.enter_context(nc.sbuf_tensor(name, shape, dt))

        def pb(name):
            return ctx.enter_context(nc.psum_tensor(name, [128, 512], fp32))

        def sem(name):
            return ctx.enter_context(nc.semaphore(name))

        ident2 = sb("ident2", [128, 128])
        minus_half2 = sb("minus_half2", [128, 1])
        oT_hi = sb("oT_hi", [128, PT, C], fp32r)
        oT_lo = sb("oT_lo", [128, PT, C], fp32r)
        x1 = [sb(f"x1{b}", [128, DM]) for b in range(2)]
        x1b = [sb(f"x1b{b}", [128, DM]) for b in range(2)]
        x1n = [sb(f"x1n{b}", [128, DM]) for b in range(2)]
        stats2 = sb("stats2", [128, 6])
        moments2 = sb("moments2", [128, 2])
        vareps2 = sb("vareps2", [128, 1])
        rstd2 = sb("rstd2", [128, 1])
        fT_hi = sb("fT_hi", [128, KT, C], fp32r)
        fT_lo = sb("fT_lo", [128, KT, C], fp32r)
        y = [sb(f"y{b}", [128, DM]) for b in range(2)]

        TO = [pb(f"TO{b}") for b in range(2)]
        TF = pb("TF")
        Y = [pb(f"Y{b}") for b in range(2)]
        F = [pb(f"F{b}") for b in range(2)]

        blank2 = sem("blank2")
        consts2_ready = sem("consts2_ready")
        oT_ready = [sem(f"oT_ready{h}") for h in range(2)]
        oT_hi_ready = [sem(f"oT_hi_ready{h}") for h in range(2)]
        oT_lo_ready = [sem(f"oT_lo_ready{h}") for h in range(2)]
        Y_ready = sem("Y_ready")
        x1_ready = sem("x1_ready")
        stats2_ready = sem("stats2_ready")
        moments2_ready = sem("moments2_ready")
        vareps2_ready = sem("vareps2_ready")
        rstd2_ready = sem("rstd2_ready")
        x1n_ready = sem("x1n_ready")
        fT_ready = sem("fT_ready")
        fT_hi_ready = sem("fT_hi_ready")
        fT_lo_ready = sem("fT_lo_ready")
        F_ready = sem("F_ready")
        y_ready = sem("y_ready")
        y_stored = sem("y_stored")

        block = ctx.enter_context(nc.Block())

        @block.sync
        def _(sp):
            def load(at, b):
                sp.dma_start(at_rows[b][:, :], attn_rows[bass.ds(at, C), :]).then_inc(rows_loaded, 16)
                sp.dma_start(x_in[b][:, :], x_rows[bass.ds(at, C), :]).then_inc(xin_loaded, 16)

            sp.wait_ge(attn_stored, 16 * NC)

            def step(i, _, b):
                one = counts(sp, i, 1, (-2, -1, 0))
                x16 = counts(sp, i, 16, (0,))
                y16 = counts(sp, i, 16, (-2,))
                before, ahead = row(sp, i - 1), row(sp, i + 1)
                if exists(i + 1):
                    wait(sp, rows_loaded, x16[0])
                    wait(sp, xin_loaded, x16[0])
                    wait(sp, oT_ready[1], one[-1])
                    wait(sp, x1_ready, one[-1])
                    load(ahead, 1 - b)
                if exists(i - 1):
                    wait(sp, y_stored, y16[-2])
                    wait(sp, y_ready, one[-1])
                    sp.dma_start(out_rows[bass.ds(before, C), :], y[1 - b][:, :]).then_inc(y_stored, 16)

            steps(sp, step, 0, NC + 1)
            sp.wait_ge(y_stored, 16 * NC)

        @block.gpsimd
        def _(pool):
            pool.memset(ident2[:, :], 0.0).then_inc(blank2, 1)
            pool.memset(minus_half2[:, :], -0.5)
            pool.wait_ge(blank2, 1)
            pool.affine_select(out=ident2[:, :], in_=ident2[:, :], compare_op=ALU.not_equal, fill=1.0,
                               base=0, pattern=[[-1, 128]], channel_multiplier=1).then_inc(consts2_ready, 1)
            pool.wait_ge(consts2_ready, 1)

            def step(i, _, b):
                if exists(i):
                    one = counts(pool, i, 1, (0,))
                    pool.wait_ge(vareps2_ready, one[0])
                    pool.tensor_tensor(rstd2[:, :], vareps2[:, :], minus_half2[:, :], ALU.pow)\
                        .then_inc(rstd2_ready, 1)

            steps(pool, step, 0, NC)

        def half(h):
            return slice(PT // 2 * h, PT // 2 * (h + 1))

        def tiles(bank):
            return bank[:, :].rearrange("p (k c) -> p k c", c=C)

        @block.scalar
        def _(act):
            def rows_hi(count, h):
                act.wait_ge(oT_ready[h], count)
                act.activation(oT_hi[:, half(h), :], tiles(TO[h]), ACT.Copy).then_inc(oT_hi_ready[h], 1)

            for h in range(2):
                rows_hi(1, h)

            def step(i, _, b):
                one = counts(act, i, 1, (-1, 0, 1))
                if exists(i - 1):
                    act.wait_ge(fT_ready, one[-1])
                    act.activation(fT_hi[:, :, :], tiles(TF), ACT.Copy).then_inc(fT_hi_ready, 1)
                if exists(i + 1):
                    for h in range(2):
                        rows_hi(one[1], h)

            steps(act, step, 0, NC + 1)

        @block.vector
        def _(dve):
            def rows_lo(count, h):
                dve.wait_ge(oT_hi_ready[h], count)
                nc.vector.tensor_tensor(oT_lo[:, half(h), :], tiles(TO[h]), oT_hi[:, half(h), :].bitcast(fp32),
                                        ALU.subtract).then_inc(oT_lo_ready[h], 1)

            for h in range(2):
                rows_lo(1, h)

            def step(i, _, b):
                one = counts(dve, i, 1, (-1, 0, 1))
                x16 = counts(dve, i, 16, (0,))
                y16 = counts(dve, i, 16, (-3,))
                here = exists(i)
                if exists(i - 1):
                    dve.wait_ge(fT_hi_ready, one[-1])
                    nc.vector.tensor_tensor(fT_lo[:, :, :], tiles(TF), fT_hi[:, :, :].bitcast(fp32),
                                            ALU.subtract).then_inc(fT_lo_ready, 1)
                if here:
                    dve.wait_ge(Y_ready, one[0])
                    dve.wait_ge(xin_loaded, x16[0])
                    nc.vector.tensor_tensor(x1[b][:, :], Y[b][:, :], x_in[b][:, :], ALU.add).then_inc(x1_ready, 1)
                    dve.wait_ge(x1_ready, one[0])
                    nc.vector.bn_stats(stats2[:, :], x1[b][:, :]).then_inc(stats2_ready, 1)
                    dve.wait_ge(stats2_ready, one[0])
                    nc.vector.tensor_tensor(x1b[b][:, :], x1[b][:, :], bias_b[:, :], ALU.add)
                    nc.vector.bn_aggr(moments2[:, :], stats2[:, :]).then_inc(moments2_ready, 1)
                    dve.wait_ge(moments2_ready, one[0])
                    nc.vector.tensor_scalar(vareps2[:, :], moments2[:, 1:2], LN_EPS, None, ALU.add)\
                        .then_inc(vareps2_ready, 1)
                if exists(i + 1):
                    for h in range(2):
                        rows_lo(one[1], h)
                if here:
                    dve.wait_ge(rstd2_ready, one[0])
                    nc.vector.tensor_scalar(x1n[b][:, :], x1[b][:, :], moments2[:, 0:1], rstd2[:, :],
                                            ALU.subtract, ALU.mult).then_inc(x1n_ready, 1)
                if exists(i - 1):
                    dve.wait_ge(F_ready, one[-1])
                    if exists(i - 3):
                        wait(dve, y_stored, y16[-3])
                    nc.vector.tensor_tensor(y[1 - b][:, :], F[1 - b][:, :], x1b[1 - b][:, :], ALU.add)\
                        .then_inc(y_ready, 1)

            steps(dve, step, 0, NC + 1)

        @block.tensor
        def _(pe):
            def transpose_rows(count, count16, b):
                pe.wait_ge(rows_loaded, count16)
                for h in range(2):
                    if count is not None:
                        pe.wait_ge(oT_lo_ready[h], count)
                    for j in range(4):
                        c = 128 * (4 * h + j)
                        made = nc.tensor.transpose(TO[h][:, C * j:C * j + C], at_rows[b][:, c:c + 128], ident2[:, :])
                    made.then_inc(oT_ready[h], 1)

            pe.wait_ge(consts2_ready, 1)
            transpose_rows(None, 16, 0)

            def passes(to, parts_T, parts_w, kts, tiles_k):
                hi_T, lo_T = parts_T
                hi_w, lo_w = parts_w
                for kt in kts:
                    for n, (a, w) in enumerate(((hi_T, hi_w), (hi_T, lo_w), (lo_T, hi_w))):
                        made = nc.tensor.matmul(to[:, :], a[:, kt, :], w[:, kt, :], start=(kt == 0 and n == 0),
                                                stop=(kt == tiles_k - 1 and n == 2))
                return made

            def step(i, _, b):
                one = counts(pe, i, 1, (-2, -1, 0))
                x16 = counts(pe, i, 16, (1,))
                if exists(i):
                    for h in range(2):
                        pe.wait_ge(oT_lo_ready[h], one[0])
                    wait(pe, x1_ready, one[-2])
                    passes(Y[b], (oT_hi, oT_lo), (wo_hi, wo_lo), range(0, PT // 2), PT)
                if exists(i - 1):
                    pe.wait_ge(x1n_ready, one[-1])
                    wait(pe, fT_lo_ready, one[-2])
                    for j in range(KT):
                        made = nc.tensor.transpose(TF[:, C * j:C * j + C], x1n[1 - b][:, 128 * j:128 * j + 128],
                                                   ident2[:, :])
                    made.then_inc(fT_ready, 1)
                if exists(i):
                    passes(Y[b], (oT_hi, oT_lo), (wo_hi, wo_lo), range(PT // 2, PT), PT).then_inc(Y_ready, 1)
                if exists(i + 1):
                    transpose_rows(one[0], x16[1], 1 - b)
                if exists(i - 1):
                    pe.wait_ge(fT_lo_ready, one[-1])
                    if exists(i - 3):
                        pe.wait_ge(y_ready, counts(pe, i, 1, (-3,))[-3])
                    passes(F[1 - b], (fT_hi, fT_lo), (wf_hi, wf_lo), range(KT), KT).then_inc(F_ready, 1)

            steps(pe, step, 0, NC + 1)


def kernel(L0_attn_x, L0_attn_Wq, L0_attn_Wk, L0_attn_Wv, L0_attn_Wo, L0_attn_Wa, L0_attn_ba,
           L0_ffn_CB, L0_ffn_SCB, L0_ffn_bias):
    import numpy as np
    import concourse.bacc as bacc
    from concourse.bass_utils import run_bass_kernel_spmd

    ins = dict(x=L0_attn_x, Wq=L0_attn_Wq, Wk=L0_attn_Wk, Wv=L0_attn_Wv, Wo=L0_attn_Wo, Wa=L0_attn_Wa,
               ba=L0_attn_ba, CBT=np.asarray(L0_ffn_CB).T, SCB=L0_ffn_SCB, bias=L0_ffn_bias)
    nc = bacc.Bacc("TRN2", target_bir_lowering=False, num_devices=1)
    arrays, args = {}, {}
    for name, a in ins.items():
        a = np.ascontiguousarray(a)
        arrays[f"in_{name}"] = a
        args[name] = nc.dram_tensor(f"in_{name}", a.shape, mybir.dt.from_np(a.dtype), kind="ExternalInput").ap()
    shape = arrays["in_x"].shape
    args["out"] = nc.dram_tensor("out_rows", shape, mybir.dt.float32, kind="ExternalOutput").ap()
    gated_linear_attention_block(nc, **args)
    got = run_bass_kernel_spmd(nc, [arrays], core_ids=[0])
    return got.results[0]["out_rows"]
```

```python
import concourse.bass as bass
from concourse import mybir
from contextlib import ExitStack


def gated_linear_attention_block(
    nc: bass.Bass,
    x: bass.AP,
    xT: bass.AP,
    Wq: bass.AP,
    Wk: bass.AP,
    Wv: bass.AP,
    Wo: bass.AP,
    Wa: bass.AP,
    ba: bass.AP,
    CBT: bass.AP,
    SCB: bass.AP,
    bias: bass.AP,
    out: bass.AP,
):
    fp32 = mybir.dt.float32
    fp32r = mybir.dt.float32r
    ALU = mybir.AluOpType
    ACT = mybir.ActivationFunctionType

    B, N, DM = x.shape
    P = Wq.shape[1]
    H = Wa.shape[1]
    DH = P // H
    E = DH + 1
    C = 128
    NC = B * N // C
    CB_ = N // C
    KT = DM // 128
    PT = P // 128
    U = 512
    NP = P // U
    NU = 3 * NP
    QT = U // (2 * C)
    NQ = PT // QT
    HU = U // DH
    GH = 4
    NG = H // GH
    LN_EPS = 1e-5
    DEN_EPS = 1e-6
    SHIFT = 2.0
    FIRST, LAST = 4, NC - 4

    x_rows = x.rearrange("b n d -> (b n) d")
    out_rows = out.rearrange("b n d -> (b n) d")
    xT_rows = xT.rearrange("q d c -> (q d) c")
    attn_rows = nc.dram_tensor("attn_rows", [NC * C, P], fp32).ap()
    decay_rows = nc.dram_tensor("decay_rows", [2, H * C + H], fp32).ap()
    norm_rows = nc.dram_tensor("norm_rows", [C, 4], fp32).ap()

    def slab(u):
        w = (Wq, Wk, Wv)[u * U // P]
        c = u * U % P
        return w[:, c:c + U].rearrange("(k p) n -> p k n", p=128)

    def row(eng, n):
        if isinstance(n, int):
            return n * C
        at = eng.snap(n * C)
        eng.compute_val(at)
        return at

    def exists(n):
        return not isinstance(n, int) or 0 <= n < NC

    def wait(eng, sem, value):
        if value is not None:
            eng.wait_ge(sem, value)

    def counts(eng, i, per, offsets):
        found = {}
        for d in offsets:
            if isinstance(i, int):
                found[d] = per * (i + d + 1) if i + d >= 0 else None
            else:
                found[d] = eng.snap(per * (i + d + 1))
                eng.compute_val(found[d])
        return found

    def steps(eng, step, first, last):
        for i in range(first, FIRST):
            step(i, i // 2, i % 2)
        with eng.Fori(FIRST // 2, LAST // 2) as r:
            for b in range(2):
                step(2 * r + b, r, b)
        for i in range(LAST, last):
            step(i, i // 2, i % 2)

    with ExitStack() as ctx:
        def sb(name, shape, dt=fp32):
            return ctx.enter_context(nc.sbuf_tensor(name, shape, dt))

        def pb(name):
            return ctx.enter_context(nc.psum_tensor(name, [128, 512], fp32))

        def sem(name):
            return ctx.enter_context(nc.semaphore(name))

        w_hi = sb("w_hi", [128, NU, KT, U], fp32r)
        w_lo = sb("w_lo", [128, NU, KT, U], fp32r)
        scale = sb("scale", [128, DM])
        bias_b = sb("bias_b", [128, DM])
        at_rows = [sb(f"at_rows{b}", [128, P]) for b in range(2)]
        x_in = [sb(f"x_in{b}", [128, DM]) for b in range(2)]
        wa_raw = sb("wa_raw", [128, KT, H])
        wa_hi = sb("wa_hi", [128, KT, H], fp32r)
        wa_lo = sb("wa_lo", [128, KT, H], fp32r)
        xt = [sb(f"xt{b}", [128, DM]) for b in range(2)]
        xT_in = sb("xT_in", [128, KT, 2 * C])
        norm_b = bias_b[:, :].rearrange("p (c s a) -> p a s c", s=2, a=2)
        stats = sb("stats", [128, 2, 6])
        moments = sb("moments", [128, 2, 2])
        vareps = sb("vareps", [128, 2])
        minus_half = sb("minus_half", [128, 2])
        xT_hi = sb("xT_hi", [128, KT, 2 * C], fp32r)
        xT_lo = sb("xT_lo", [128, KT, 2 * C], fp32r)
        relu_t = [sb(f"relu_t{b}", [128, U]) for b in range(2)]
        exp_t = [sb(f"exp_t{b}", [128, U]) for b in range(2)]
        k = [sb(f"k{b}", [128, P]) for b in range(2)]
        v1 = [sb(f"v1{b}", [128, H, E]) for b in range(2)]
        vw = sb("vw", [128, H, E])
        qT = sb("qT", [128, PT, 2 * C])
        kT = sb("kT", [128, PT, C])
        ident = sb("ident", [128, 128])
        eye4 = sb("eye4", [128, GH, C])
        zeros = sb("zeros", [H, C])
        keep = sb("keep", [H, NC])
        ba_c = sb("ba_c", [H, 1])
        minus_ba = sb("minus_ba", [H, 1])
        exp_z = sb("exp_z", [H, C])
        one_exp = sb("one_exp", [H, C])
        aT = sb("aT", [H, C])
        pT = sb("pT", [H, C])
        p_tok = [sb(f"p_tok{b}", [128, H]) for b in range(2)]
        abc = sb("abc", [128, H * C])
        pc = [sb(f"pc{b}", [128, H]) for b in range(2)]
        D = sb("D", [128, H, C])
        M = sb("M", [128, 2 * GH, C])
        S = sb("S", [128, PT, 2, E])
        num = sb("num", [128, H, E])
        den = sb("den", [128, H])
        rden = sb("rden", [128, H])
        attn = sb("attn", [128, P])

        def pieces(t, n):
            dims = " ".join("abc"[:len(t.shape) - 1])
            flat = t[tuple(slice(None) for _ in t.shape)].rearrange(f"p {dims} -> p ({dims})")
            return [flat[:, U * j:U * j + U] for j in range(n)]

        order = [NP, NP + 1, 0, 1, 2 * NP, 2 * NP + 1]
        raw = pieces(D, 4) + pieces(abc, 4) + pieces(at_rows[0], 2) + pieces(at_rows[1], 2) + pieces(k[1], 2) \
            + pieces(x_in[0], 1) + pieces(x_in[1], 1) + pieces(M, 2) + pieces(attn, 2) + pieces(num, 2) + pieces(vw, 2)

        wo_hi, wo_lo = (w[:, 0:PT // KT, :, :].rearrange("p u k n -> p (u k) n") for w in (w_hi, w_lo))
        wf_hi, wf_lo = (w[:, PT // KT, :, :] for w in (w_hi, w_lo))
        oT_hi, oT_lo = (w[:, 3, 0:2, :].rearrange("p k (j c) -> p (k j) c", c=C) for w in (w_hi, w_lo))
        fT_hi, fT_lo = (w[:, 3, 2, :].rearrange("p (j c) -> p j c", c=C) for w in (w_hi, w_lo))
        x1 = [t[:, :] for t in relu_t]
        x1b = [t[:, :] for t in exp_t]
        x1n = pieces(k[NC % 2], 2)
        y = [t[:, :] for t in xt]
        raw_wo = pieces(at_rows[0], 2) + pieces(x_in[0], 1) + pieces(x_in[1], 1) + pieces(at_rows[1], 2) \
            + pieces(xt[0], 1) + pieces(xt[1], 1)
        raw_wf = pieces(abc, KT)
        stats2 = sb("stats2", [128, 6])
        moments2 = sb("moments2", [128, 2])
        vareps2 = sb("vareps2", [128, 1])
        rstd2 = sb("rstd2", [128, 1])

        G = [pb(f"G{b}") for b in range(2)]
        T = [pb(f"T{b}") for b in range(2)]
        SC = [pb(f"SC{b}") for b in range(2)]
        PV = pb("PV")
        IN = pb("IN")
        DELTA = GH * E
        TO = T[::-1]
        TF = SC[0]
        Y = G
        F = [SC[1], PV]

        raw_loaded = [sem(f"raw_loaded{u}") for u in range(NU)]
        scale_loaded = sem("scale_loaded")
        scaled = sem("scaled")
        wo_loaded = [sem(f"wo_loaded{u}") for u in range(PT // KT)]
        wf_loaded = sem("wf_loaded")
        wf_scaled = sem("wf_scaled")
        wo_hi_ready = sem("wo_hi_ready")
        wo_lo_ready = sem("wo_lo_ready")
        wf_hi_ready = sem("wf_hi_ready")
        wf_lo_ready = sem("wf_lo_ready")
        rows_loaded = sem("rows_loaded")
        xin_loaded = sem("xin_loaded")
        attn_stored = sem("attn_stored")
        small_loaded = sem("small_loaded")
        w_hi_ready = sem("w_hi_ready")
        w_lo_ready = sem("w_lo_ready")
        wa_ready = sem("wa_ready")
        blank = sem("blank")
        consts_ready = sem("consts_ready")
        ba_ready = sem("ba_ready")
        x_loaded = [sem(f"x_loaded{b}") for b in range(2)]
        xT_loaded = sem("xT_loaded")
        norm_stored = sem("norm_stored")
        norm_loaded = sem("norm_loaded")
        bias_loaded = sem("bias_loaded")
        xT_centred = sem("xT_centred")
        xT_normal = sem("xT_normal")
        stats_ready = sem("stats_ready")
        moments_ready = sem("moments_ready")
        vareps_ready = sem("vareps_ready")
        rstd_ready = sem("rstd_ready")
        xn_ready = sem("xn_ready")
        xnT_ready = [sem(f"xnT_ready{b}") for b in range(2)]
        xT_hi_ready = [sem(f"xT_hi_ready{b}") for b in range(2)]
        xT_lo_ready = [sem(f"xT_lo_ready{b}") for b in range(2)]
        k_unit_ready = [sem(f"k_unit_ready{j}") for j in range(NP)]
        q_unit_ready = [sem(f"q_unit_ready{u}") for u in range(NQ)]
        v_unit_ready = [sem(f"v_unit_ready{j}") for j in range(NP)]
        exp_k_ready = [sem(f"exp_k_ready{j}") for j in range(NP)]
        exp_q_ready = [sem(f"exp_q_ready{u}") for u in range(NQ)]
        k_ready = [sem(f"k_ready{j}") for j in range(NP)]
        q_ready = [sem(f"q_ready{u}") for u in range(NQ)]
        kT_ready = [sem(f"kT_ready{j}") for j in range(NP)]
        kT_copied = [sem(f"kT_copied{j}") for j in range(NP)]
        v_ready = [sem(f"v_ready{j}") for j in range(NP)]
        z_ready = sem("z_ready")
        exp_z_ready = sem("exp_z_ready")
        one_exp_ready = sem("one_exp_ready")
        a_ready = sem("a_ready")
        pT_ready = sem("pT_ready")
        decay_ready = sem("decay_ready")
        decay_stored = sem("decay_stored")
        abc_loaded = sem("abc_loaded")
        p_ready = sem("p_ready")
        p_copied = sem("p_copied")
        D_ready = sem("D_ready")
        vw_ready = sem("vw_ready")
        scores_ready = [sem(f"scores_ready{r}") for r in range(2)]
        M_ready = [sem(f"M_ready{r}") for r in range(2)]
        group_ready = [sem(f"group_ready{g}") for g in range(NG)]
        inter_scaled = [sem(f"inter_scaled{g}") for g in range(NG)]
        group_done = [sem(f"group_done{g}") for g in range(NG)]
        den_ready = sem("den_ready")
        rden_ready = sem("rden_ready")
        attn_ready = sem("attn_ready")

        oT_ready = [sem(f"oT_ready{h}") for h in range(2)]
        oT_hi_ready = [sem(f"oT_hi_ready{h}") for h in range(2)]
        oT_lo_ready = [sem(f"oT_lo_ready{h}") for h in range(2)]
        Y_ready = sem("Y_ready")
        x1_ready = sem("x1_ready")
        stats2_ready = sem("stats2_ready")
        moments2_ready = sem("moments2_ready")
        vareps2_ready = sem("vareps2_ready")
        rstd2_ready = sem("rstd2_ready")
        x1n_ready = sem("x1n_ready")
        fT_ready = sem("fT_ready")
        fT_hi_ready = sem("fT_hi_ready")
        fT_lo_ready = sem("fT_lo_ready")
        F_ready = sem("F_ready")
        y_ready = sem("y_ready")
        y_stored = sem("y_stored")

        block = ctx.enter_context(nc.Block())

        def z_bank():
            return T[0]

        def kT_bank(j, a_odd):
            return T[j] if a_odd else T[1 - j]

        def p_bank(a_odd):
            return T[0] if a_odd else T[1]

        def xT_bank(s):
            return T[s]

        def tokens(s):
            return slice(C * s, C * s + C)

        def tiles_of(bank):
            return bank[:, :].rearrange("p (k c) -> p k c", c=C)

        def half(h):
            return slice(PT // 2 * h, PT // 2 * (h + 1))

        @block.sync
        def _(sp):
            for s in range(2):
                sp.dma_start(xt[s][:, :], x_rows[C * s:C * s + C, :]).then_inc(x_loaded[s], 16)
            sp.dma_start(wa_raw[:, :, :], Wa.rearrange("(k p) h -> p k h", p=128)).then_inc(small_loaded, 16)
            sp.dma_start(ba_c[:, :], ba.rearrange("(h a) -> h a", a=1)).then_inc(small_loaded, 16)
            for n, u in enumerate(order):
                for kt in range(KT):
                    sp.dma_start(raw[KT * n + kt], slab(u)[:, kt, :]).then_inc(raw_loaded[n], 16)
            sp.dma_start(scale[:, :], SCB.rearrange("(a n) -> a n", a=1).broadcast_to([128, DM]))\
                .then_inc(scale_loaded, 16)

            def output_weights():
                sp.wait_ge(w_lo_ready, NU * KT)
                sp.wait_ge(stats_ready, NC // 2)
                for kt in range(PT):
                    sp.dma_start(raw_wo[kt], Wo[128 * kt:128 * kt + 128, :]).then_inc(wo_loaded[kt // KT], 16)

            def ffn_weights():
                sp.wait_ge(D_ready, NC)
                for kt in range(KT):
                    sp.dma_start(raw_wf[kt], CBT[128 * kt:128 * kt + 128, :]).then_inc(wf_loaded, 16)
                sp.wait_ge(xT_normal, NC // 2 - 1)
                sp.dma_start(bias_b[:, :], bias.rearrange("(a n) -> a n", a=1).broadcast_to([128, DM]))\
                    .then_inc(bias_loaded, 16)

            def load(at, b):
                sp.dma_start(at_rows[b][:, :], attn_rows[bass.ds(at, C), :]).then_inc(rows_loaded, 16)
                sp.dma_start(x_in[b][:, :], x_rows[bass.ds(at, C), :]).then_inc(xin_loaded, 16)

            def step(i, pair, b):
                one = counts(sp, i, 1, (-2, -1, 0, 1))
                pairs = counts(sp, pair, 1, (0, 1, 2))
                p16 = counts(sp, pair, 16, (1,))
                d32 = counts(sp, i, 32, (1,))
                normal = b == 1 and exists(i + 3)
                here = row(sp, i)
                if normal:
                    for s in range(2):
                        later = row(sp, i + 3 + s)
                        if exists(i):
                            sp.wait_ge(stats_ready, pairs[1])
                        else:
                            sp.wait_ge(xnT_ready[s], 1)
                        sp.dma_start(xt[s][:, :], x_rows[bass.ds(later, C), :]).then_inc(x_loaded[s], 16)
                    if exists(i):
                        sp.wait_ge(xT_lo_ready[1], pairs[1])
                    at = (pair + 2) * DM
                    if not isinstance(pair, int):
                        at = sp.snap(at)
                        sp.compute_val(at)
                    sp.dma_start(xT_in[:, :, :], xT_rows[bass.ds(at, DM), :].rearrange("(k p) c -> p k c", p=128))\
                        .then_inc(xT_loaded, 16)
                if isinstance(i, int) and i == NC - 3:
                    output_weights()
                if exists(i + 1):
                    decays = decay_rows[1 - b, :]
                    wait(sp, decay_ready, one[1])
                    sp.dma_start(decays[0:H * C].rearrange("(h c) -> h c", h=H), aT[:, :]).then_inc(decay_stored, 16)
                    sp.dma_start(decays[H * C:H * C + H].rearrange("(h c) -> h c", h=H),
                                 pT[:, C - 1:C]).then_inc(decay_stored, 16)
                    sp.wait_ge(decay_stored, d32[1])
                    if not exists(i):
                        sp.wait_ge(w_lo_ready, 2 * KT)
                    wait(sp, D_ready, one[0])
                    sp.dma_start(abc[:, :], decays[0:H * C].rearrange("(a n) -> a n", a=1)
                                 .broadcast_to([128, H * C])).then_inc(abc_loaded, 16)
                    sp.dma_start(pc[1 - b][:, :], decays[H * C:H * C + H].rearrange("(a n) -> a n", a=1)
                                 .broadcast_to([128, H])).then_inc(abc_loaded, 16)
                if normal:
                    sp.wait_ge(rstd_ready, pairs[2])
                    wait(sp, xT_normal, pairs[0])
                    sp.dma_start(norm_rows, moments[:, :, :].rearrange("p s a -> p (s a)")).then_inc(norm_stored, 16)
                    sp.wait_ge(norm_stored, p16[1])
                    sp.dma_start(bias_b[:, :], norm_rows.rearrange("(q c) m -> q (c m)", q=1).broadcast_to([128, 4 * C]))\
                        .then_inc(norm_loaded, 16)
                if isinstance(i, int) and i == NC - 2:
                    sp.wait_ge(attn_stored, 16 * 3)
                    sp.wait_ge(wo_lo_ready, KT)
                    load(0, 0)
                    ffn_weights()
                if isinstance(i, int) and i == NC - 1:
                    sp.wait_ge(wo_lo_ready, PT)
                    sp.wait_ge(rows_loaded, 16)
                    sp.wait_ge(xin_loaded, 16)
                    load(C, 1)
                    sp.wait_ge(rows_loaded, 32)
                    sp.wait_ge(xin_loaded, 32)
                    sp.wait_ge(oT_ready[1], 1)
                    sp.wait_ge(x1_ready, 1)
                    load(2 * C, 0)
                if exists(i):
                    wait(sp, attn_ready, one[0])
                    sp.dma_start(attn_rows[bass.ds(here, C), :], attn[:, :]).then_inc(attn_stored, 16)

            steps(sp, step, -1, NC)

            def step2(i, _, b):
                one = counts(sp, i, 1, (-2, -1))
                x16 = counts(sp, i, 16, (0,))
                y16 = counts(sp, i, 16, (-3,))
                before, ahead = row(sp, i - 2), row(sp, i + 1)
                if isinstance(i, int) and i == 2:
                    sp.wait_ge(attn_stored, 16 * NC)
                if exists(i + 1) and exists(i - 2):
                    wait(sp, rows_loaded, x16[0])
                    wait(sp, xin_loaded, x16[0])
                    wait(sp, oT_ready[1], one[-1])
                    wait(sp, x1_ready, one[-1])
                    load(ahead, 1 - b)
                if exists(i - 2):
                    wait(sp, y_stored, y16[-3])
                    wait(sp, y_ready, one[-2])
                    sp.dma_start(out_rows[bass.ds(before, C), :], y[b]).then_inc(y_stored, 16)

            steps(sp, step2, 1, NC + 2)
            sp.wait_ge(y_stored, 16 * NC)

        @block.gpsimd
        def _(pool):
            pool.memset(ident[:, :], 0.0).then_inc(blank, 1)
            pool.memset(eye4[:, :, :], 0.0).then_inc(blank, 1)
            pool.memset(keep[:, :], 1.0).then_inc(blank, 1)
            pool.memset(minus_half[:, :], -0.5)
            pool.memset(zeros[:, :], 0.0)
            pool.memset(S[:, :, :, :], 0.0)
            for b in range(2):
                pool.memset(v1[b][:, :, DH:E], 1.0)
            pool.wait_ge(blank, 3)
            pool.memset(keep[:, 0:NC:CB_], 0.0)
            pool.affine_select(out=ident[:, :], in_=ident[:, :], compare_op=ALU.not_equal, fill=1.0,
                               base=0, pattern=[[-1, 128]], channel_multiplier=1)
            pool.affine_select(out=eye4[:, :, :], in_=eye4[:, :, :], compare_op=ALU.not_equal, fill=1.0,
                               base=0, pattern=[[0, GH], [-1, C]], channel_multiplier=1)\
                .then_inc(consts_ready, 1)

            def inverse_deviation(count):
                pool.wait_ge(vareps_ready, count)
                pool.tensor_tensor(moments[:, :, 1], vareps[:, :], minus_half[:, :], ALU.pow).then_inc(rstd_ready, 1)

            def inverse_deviation2(count):
                pool.wait_ge(vareps2_ready, count)
                pool.tensor_tensor(rstd2[:, :], vareps2[:, :], minus_half[:, 0:1], ALU.pow).then_inc(rstd2_ready, 1)

            def step(i, pair, b):
                if b == 1 and exists(i + 3):
                    pairs = counts(pool, pair, 1, (1, 2))
                    p16 = counts(pool, pair, 16, (1,))
                    inverse_deviation(pairs[2])
                    x4 = xT_in[:, :, :].rearrange("p k (s c) -> p k s c", s=2)
                    pool.wait_ge(xT_loaded, p16[1])
                    pool.wait_ge(norm_loaded, p16[1])
                    pool.tensor_tensor(x4, x4, norm_b[:, 0:1, :, :].broadcast_to([128, KT, 2, C]), ALU.subtract)\
                       .then_inc(xT_centred, 1)
                    pool.wait_ge(xT_centred, pairs[1])
                    pool.tensor_tensor(x4, x4, norm_b[:, 1:2, :, :].broadcast_to([128, KT, 2, C]), ALU.mult)\
                       .then_inc(xT_normal, 1)
                if not exists(i + 1):
                    pool.wait_ge(wf_loaded, 16 * KT)
                    pool.wait_ge(scaled, 1)
                    for kt in range(KT):
                        pool.tensor_tensor(raw_wf[kt], raw_wf[kt], scale[:, :], ALU.mult).then_inc(wf_scaled, 1)
                    inverse_deviation2(1)

            def step2(i, _, b):
                if exists(i):
                    inverse_deviation2(counts(pool, i, 1, (0,))[0])

            pool.wait_ge(consts_ready, 1)
            inverse_deviation(1)
            steps(pool, step, -1, NC)
            steps(pool, step2, 1, NC)

        @block.scalar
        def _(act):
            def first_x_hi(s):
                act.wait_ge(xnT_ready[s], 1)
                act.activation(xT_hi[:, :, tokens(s)], tiles_of(xT_bank(s)), ACT.Copy).then_inc(xT_hi_ready[s], 1)

            def x_hi(s, count, used):
                act.wait_ge(xT_normal, count)
                act.wait_ge(v_unit_ready[NP - 1], used)
                act.activation(xT_hi[:, :, tokens(s)], xT_in[:, :, tokens(s)], ACT.Copy).then_inc(xT_hi_ready[s], 1)

            def split_hi(n):
                act.wait_ge(raw_loaded[n], 16 * KT)
                for kt in range(KT):
                    act.activation(w_hi[:, order[n], kt, :], raw[KT * n + kt], ACT.Copy).then_inc(w_hi_ready, 1)

            act.wait_ge(small_loaded, 32)
            act.activation(wa_hi[:, :, :], wa_raw[:, :, :], ACT.Copy).then_inc(w_hi_ready, 1)
            split_hi(0)
            for s in range(2):
                first_x_hi(s)
            split_hi(1)
            split_hi(2)

            def output_weights_hi(h):
                act.wait_ge(q_unit_ready[NQ - 1], NC // 2)
                act.wait_ge(wo_loaded[h], 16 * KT)
                for kt in range(KT * h, KT * h + KT):
                    act.activation(wo_hi[:, kt, :], raw_wo[kt], ACT.Copy).then_inc(wo_hi_ready, 1)

            def ffn_weights_hi():
                for kt in range(KT):
                    act.wait_ge(wf_scaled, kt + 1)
                    act.activation(wf_hi[:, kt, :], raw_wf[kt], ACT.Copy).then_inc(wf_hi_ready, 1)

            def rows_hi(count):
                for h in range(2):
                    act.wait_ge(oT_ready[h], count)
                    act.activation(oT_hi[:, half(h), :], tiles_of(TO[h]), ACT.Copy).then_inc(oT_hi_ready[h], 1)

            def step(i, pair, b):
                one = counts(act, i, 1, (0, 1))
                pairs = counts(act, pair, 1, (0, 1))
                start = not exists(i)
                if not exists(i + 1):
                    ffn_weights_hi()
                    rows_hi(2)
                    return
                o = 1 - b

                def elu_parts(j, made, made_count, used, used_count, ready):
                    act.wait_ge(made, made_count)
                    wait(act, used, used_count)
                    act.activation(relu_t[j][:, :], G[j][:, :], ACT.Relu)
                    act.activation(exp_t[j][:, :], G[j][:, :], ACT.Exp).then_inc(ready, 1)

                def k_parts(j):
                    if b == 1:
                        elu_parts(j, k_unit_ready[j], one[1], k_ready[j], one[0], exp_k_ready[j])
                    else:
                        elu_parts(j, k_unit_ready[j], one[1], q_ready[NQ - 2 + j], pairs[0], exp_k_ready[j])

                def q_parts(u):
                    if u < 2:
                        elu_parts(u, q_unit_ready[u], pairs[1], k_ready[u], one[1], exp_q_ready[u])
                    else:
                        elu_parts(u % 2, q_unit_ready[u], pairs[1], q_ready[u - 2], pairs[1], exp_q_ready[u])

                def copy_kT(j):
                    act.wait_ge(kT_ready[j], one[1])
                    act.activation(kT[:, 4 * j:4 * j + 4, :], tiles_of(kT_bank(j, o)), ACT.Copy)\
                        .then_inc(kT_copied[j], 1)

                def copy_v(j):
                    act.wait_ge(v_unit_ready[j], one[1])
                    act.activation(v1[o][:, HU * j:HU * j + HU, 0:DH],
                                   G[j][:, :].rearrange("p (h d) -> p h d", h=HU), ACT.Copy).then_inc(v_ready[j], 1)

                def exp_logits():
                    act.wait_ge(z_ready, one[1])
                    if start:
                        act.wait_ge(ba_ready, 1)
                    wait(act, one_exp_ready, one[0])
                    act.activation(exp_z[:, :], z_bank()[0:H, 0:C], ACT.Exp,
                                   bias=minus_ba[:, :], scale=-1.0).then_inc(exp_z_ready, 1)

                def copy_p():
                    act.wait_ge(p_ready, one[1])
                    act.activation(p_tok[o][:, :], p_bank(o)[:, 0:H], ACT.Copy).then_inc(p_copied, 1)

                if b == 0 and exists(i + 2):
                    x_hi(0, pairs[0], one[0])
                k_parts(0)
                exp_logits()
                k_parts(1)
                if b == 1:
                    if start:
                        split_hi(3)
                    q_parts(0)
                    if start:
                        split_hi(4)
                    q_parts(1)
                    copy_kT(0)
                    if start:
                        split_hi(5)
                    q_parts(2)
                    copy_kT(1)
                    copy_p()
                    q_parts(3)
                    copy_v(0)
                    copy_v(1)
                    if isinstance(i, int) and i == NC - 3:
                        output_weights_hi(0)
                else:
                    copy_v(0)
                    if isinstance(i, int) and i == NC - 2:
                        output_weights_hi(1)
                    copy_kT(0)
                    copy_kT(1)
                    copy_v(1)
                    if exists(i + 2):
                        x_hi(1, pairs[0], one[1])
                    copy_p()
                    if isinstance(i, int) and i == NC - 2:
                        rows_hi(1)

            steps(act, step, -1, NC)

            def step2(i, _, b):
                one = counts(act, i, 1, (-1, 1))
                act.wait_ge(fT_ready, one[-1])
                act.activation(fT_hi[:, :, :], tiles_of(TF), ACT.Copy).then_inc(fT_hi_ready, 1)
                if exists(i + 1):
                    rows_hi(one[1])

            steps(act, step2, 1, NC + 1)

        @block.vector
        def _(dve):
            def x_stats(count16):
                for s in range(2):
                    dve.wait_ge(x_loaded[s], count16)
                    made = nc.vector.bn_stats(stats[:, s, :], xt[s][:, :])
                made.then_inc(stats_ready, 1)

            def x_moments(count):
                for s in range(2):
                    made = nc.vector.bn_aggr(moments[:, s, :], stats[:, s, :])
                made.then_inc(moments_ready, 1)
                dve.wait_ge(moments_ready, count)
                nc.vector.tensor_scalar(vareps[:, :], moments[:, :, 1], LN_EPS, None, ALU.add)\
                    .then_inc(vareps_ready, 1)

            def first_x_normal():
                dve.wait_ge(rstd_ready, 1)
                for s in range(2):
                    made = nc.vector.tensor_scalar(xt[s][:, :], xt[s][:, :], moments[:, s, 0:1], moments[:, s, 1:2],
                                                   ALU.subtract, ALU.mult)
                made.then_inc(xn_ready, 1)

            def x_lo(s, count, whole):
                dve.wait_ge(xT_hi_ready[s], count)
                nc.vector.tensor_tensor(xT_lo[:, :, tokens(s)], whole, xT_hi[:, :, tokens(s)].bitcast(fp32),
                                        ALU.subtract).then_inc(xT_lo_ready[s], 1)

            def split_lo(n):
                for kt in range(KT):
                    dve.wait_ge(w_hi_ready, KT * n + kt + 2)
                    nc.vector.tensor_tensor(w_lo[:, order[n], kt, :], raw[KT * n + kt],
                                            w_hi[:, order[n], kt, :].bitcast(fp32), ALU.subtract).then_inc(w_lo_ready, 1)

            x_stats(16)
            dve.wait_ge(small_loaded, 32)
            dve.wait_ge(stats_ready, 1)
            nc.vector.tensor_scalar(minus_ba[:, :], ba_c[:, :], -1.0, -SHIFT, ALU.mult, ALU.add).then_inc(ba_ready, 1)
            x_moments(1)
            dve.wait_ge(w_hi_ready, 1)
            nc.vector.tensor_tensor(wa_lo[:, :, :], wa_raw[:, :, :], wa_hi[:, :, :].bitcast(fp32),
                                    ALU.subtract).then_inc(wa_ready, 1)
            first_x_normal()
            split_lo(0)
            for s in range(2):
                x_lo(s, 1, tiles_of(xT_bank(s)))
            split_lo(1)
            split_lo(2)

            def output_weights_lo(h):
                for kt in range(KT * h, KT * h + KT):
                    dve.wait_ge(wo_hi_ready, kt + 1)
                    nc.vector.tensor_tensor(wo_lo[:, kt, :], raw_wo[kt], wo_hi[:, kt, :].bitcast(fp32),
                                            ALU.subtract).then_inc(wo_lo_ready, 1)

            def ffn_weights_lo():
                for kt in range(KT):
                    dve.wait_ge(wf_hi_ready, kt + 1)
                    nc.vector.tensor_tensor(wf_lo[:, kt, :], raw_wf[kt], wf_hi[:, kt, :].bitcast(fp32),
                                            ALU.subtract).then_inc(wf_lo_ready, 1)

            def rows_lo(count):
                for h in range(2):
                    dve.wait_ge(oT_hi_ready[h], count)
                    nc.vector.tensor_tensor(oT_lo[:, half(h), :], tiles_of(TO[h]), oT_hi[:, half(h), :].bitcast(fp32),
                                            ALU.subtract).then_inc(oT_lo_ready[h], 1)

            def residual(count, count16, b):
                dve.wait_ge(Y_ready, count)
                dve.wait_ge(xin_loaded, count16)
                nc.vector.tensor_tensor(x1[b], Y[b][:, :], x_in[b][:, :], ALU.add).then_inc(x1_ready, 1)
                dve.wait_ge(x1_ready, count)
                nc.vector.bn_stats(stats2[:, :], x1[b]).then_inc(stats2_ready, 1)

            def residual_rest(count, b):
                dve.wait_ge(stats2_ready, count)
                nc.vector.tensor_tensor(x1b[b], x1[b], bias_b[:, :], ALU.add)
                nc.vector.bn_aggr(moments2[:, :], stats2[:, :]).then_inc(moments2_ready, 1)
                dve.wait_ge(moments2_ready, count)
                nc.vector.tensor_scalar(vareps2[:, :], moments2[:, 1:2], LN_EPS, None, ALU.add)\
                    .then_inc(vareps2_ready, 1)

            def residual_normal(count, b):
                dve.wait_ge(rstd2_ready, count)
                nc.vector.tensor_scalar(x1n[b], x1[b], moments2[:, 0:1], rstd2[:, :],
                                        ALU.subtract, ALU.mult).then_inc(x1n_ready, 1)

            dve.wait_ge(consts_ready, 1)

            def step(i, pair, b):
                one = counts(dve, i, 1, (-1, 0, 1))
                pairs = counts(dve, pair, 1, (1, 2))
                p16 = counts(dve, pair, 16, (0, 2))
                d32 = counts(dve, i, 32, (0, 1))
                a16 = counts(dve, i, 16, (-1,))
                start = not exists(i)
                here = exists(i)
                ahead = exists(i + 1)
                wide = b == 1 and ahead
                normal = b == 1 and exists(i + 3)
                o = 1 - b

                def normalised(count, stored):
                    dve.wait_ge(group_done[NG - 1], count)
                    nc.vector.tensor_scalar(den[:, :], num[:, :, DH], DEN_EPS, None, ALU.add).then_inc(den_ready, 1)
                    dve.wait_ge(den_ready, count)
                    nc.vector.reciprocal(rden[:, :], den[:, :]).then_inc(rden_ready, 1)
                    wait(dve, attn_stored, stored)
                    dve.wait_ge(rden_ready, count)
                    nc.vector.tensor_tensor(attn[:, :].rearrange("p (h d) -> p h d", h=H), num[:, :, 0:DH],
                                            rden[:, :].rearrange("p (h a) -> p h a", a=1)
                                            .broadcast_to([128, H, DH]), ALU.mult).then_inc(attn_ready, 1)

                def elu_k(j):
                    dve.wait_ge(exp_k_ready[j], one[1])
                    nc.vector.scalar_tensor_tensor(k[o][:, U * j:U * j + U], exp_t[j][:, :], 1.0, relu_t[j][:, :],
                                                   ALU.min, ALU.add).then_inc(k_ready[j], 1)

                def elu_q(u):
                    dve.wait_ge(exp_q_ready[u], pairs[1])
                    wait(dve, group_ready[u], one[0])
                    nc.vector.scalar_tensor_tensor(qT[:, QT * u:QT * u + QT, :].rearrange("p k c -> p (k c)"),
                                                   exp_t[u % 2][:, :], 1.0, relu_t[u % 2][:, :],
                                                   ALU.min, ALU.add).then_inc(q_ready[u], 1)

                def masked(r):
                    dve.wait_ge(scores_ready[r], one[0])
                    for e in range(2):
                        made = nc.vector.tensor_tensor(
                            M[:, e:2 * GH:2, :], SC[e][:, :].rearrange("p (h c) -> p h c", h=GH),
                            D[:, 2 * GH * r + e:2 * GH * (r + 1):2, :], ALU.mult)
                    made.then_inc(M_ready[r], 1)

                def group(g):
                    hs = slice(GH * g, GH * g + GH)
                    dve.wait_ge(group_ready[g], one[0])
                    nc.vector.tensor_tensor(num[:, hs, :], IN[:, 0:DELTA].rearrange("p (h e) -> p h e", h=GH),
                                            p_tok[b][:, hs].rearrange("p (h a) -> p h a", a=1)
                                            .broadcast_to([128, GH, E]), ALU.mult).then_inc(inter_scaled[g], 1)
                    for j in range(GH):
                        h = GH * g + j
                        ps = slice(64 * (h % 2), 64 * (h % 2) + 64)
                        c = DELTA + E * (j // 2)
                        nc.vector.scalar_tensor_tensor(S[ps, h // 2, h % 2, :], S[ps, h // 2, h % 2, :],
                                                       pc[b][ps, h:h + 1], IN[ps, c:c + E], ALU.mult, ALU.add)
                    dve.wait_ge(inter_scaled[g], one[0])
                    nc.vector.tensor_tensor(num[:, hs, :], num[:, hs, :],
                                            PV[:, 0:DELTA].rearrange("p (h e) -> p h e", h=GH),
                                            ALU.add).then_inc(group_done[g], 1)

                def decay_matrix(j):
                    made = nc.vector.tensor_tensor_scan(
                        D[:, GH * j:GH * j + GH, :].rearrange("p h c -> p (h c)"),
                        abc[:, GH * j * C:GH * (j + 1) * C],
                        eye4[:, :, :].rearrange("p h c -> p (h c)"), 0.0, ALU.mult, ALU.add)
                    if j == NG - 1:
                        made.then_inc(D_ready, 1)

                if ahead:
                    elu_k(0)
                if here:
                    dve.wait_ge(D_ready, one[0])
                    masked(0)
                if not ahead:
                    normalised(one[-1], 16 * (NC - 2))
                if ahead:
                    dve.wait_ge(exp_z_ready, one[1])
                    nc.vector.tensor_scalar(one_exp[:, :], exp_z[:, :], 1.0, None, ALU.add).then_inc(one_exp_ready, 1)
                    wait(dve, decay_stored, d32[0])
                    wait(dve, p_ready, one[0])
                    dve.wait_ge(one_exp_ready, one[1])
                    nc.vector.reciprocal(aT[:, :], one_exp[:, :]).then_inc(a_ready, 1)
                    elu_k(1)
                    dve.wait_ge(a_ready, one[1])
                    nc.vector.tensor_tensor_scan(pT[:, :], aT[:, :], zeros[:, :], keep[:, bass.ds(i + 1, 1)],
                                                 ALU.mult, ALU.add).then_inc(pT_ready, 1)
                    dve.wait_ge(pT_ready, one[1])
                    nc.vector.memset(aT[:, 0:1], 0.0).then_inc(decay_ready, 1)
                if here:
                    dve.wait_ge(p_copied, one[0])
                    dve.wait_ge(abc_loaded, d32[0])
                    wait(dve, attn_ready, one[-1])
                    group(0)
                if not ahead:
                    output_weights_lo(1)
                if start:
                    split_lo(3)
                if wide:
                    elu_q(0)
                if normal:
                    x_stats(p16[2])
                if here:
                    group(1)
                if normal:
                    dve.wait_ge(stats_ready, pairs[2])
                    wait(dve, norm_stored, p16[0])
                if wide:
                    elu_q(1)
                if normal:
                    x_moments(pairs[2])
                if start:
                    split_lo(4)
                    split_lo(5)
                    dve.wait_ge(scale_loaded, 16)
                    nc.vector.tensor_scalar(scale[:, :], scale[:, :], 1.0 / 127.0, None, ALU.mult).then_inc(scaled, 1)
                if here:
                    masked(1)
                if not ahead:
                    ffn_weights_lo()
                if b == 0 and exists(i + 2):
                    x_lo(0, pairs[1], xT_in[:, :, tokens(0)])
                if ahead:
                    if start:
                        dve.wait_ge(w_lo_ready, NU * KT)
                    dve.wait_ge(abc_loaded, d32[1])
                    wait(dve, M_ready[0], one[0])
                    wait(dve, vw_ready, one[0])
                    decay_matrix(0)
                    decay_matrix(1)
                if here:
                    group(2)
                if not ahead:
                    rows_lo(2)
                if wide:
                    elu_q(2)
                if ahead:
                    wait(dve, M_ready[1], one[0])
                    decay_matrix(2)
                    decay_matrix(3)
                if b == 0 and exists(i + 2):
                    x_lo(1, pairs[1], xT_in[:, :, tokens(1)])
                if isinstance(i, int) and i == NC - 2:
                    rows_lo(1)
                if here:
                    group(3)
                if not ahead:
                    dve.wait_ge(bias_loaded, 16)
                    residual(1, 16, 0)
                    residual_rest(1, 0)
                if wide:
                    elu_q(3)
                if not ahead:
                    residual_normal(1, 0)
                if here and not (isinstance(i, int) and i == NC - 2):
                    normalised(one[0], a16[-1])
                if ahead:
                    dve.wait_ge(D_ready, one[1])
                    for j in range(NP):
                        dve.wait_ge(v_ready[j], one[1])
                    nc.vector.tensor_tensor(vw[:, :, :], v1[o][:, :, :], D[:, :, C - 1:C].broadcast_to([128, H, E]),
                                            ALU.mult).then_inc(vw_ready, 1)
                if isinstance(i, int) and i == NC - 3:
                    output_weights_lo(0)

            steps(dve, step, -1, NC)

            def step2(i, _, b):
                one = counts(dve, i, 1, (-1, 0, 1))
                x16 = counts(dve, i, 16, (0,))
                y16 = counts(dve, i, 16, (-3,))
                dve.wait_ge(fT_hi_ready, one[-1])
                nc.vector.tensor_tensor(fT_lo[:, :, :], tiles_of(TF), fT_hi[:, :, :].bitcast(fp32),
                                        ALU.subtract).then_inc(fT_lo_ready, 1)
                if exists(i):
                    residual(one[0], x16[0], b)
                if exists(i + 1):
                    rows_lo(one[1])
                if exists(i):
                    residual_rest(one[0], b)
                    residual_normal(one[0], b)
                dve.wait_ge(F_ready, one[-1])
                if exists(i - 3):
                    wait(dve, y_stored, y16[-3])
                nc.vector.tensor_tensor(y[1 - b], F[1 - b][:, :], x1b[1 - b], ALU.add).then_inc(y_ready, 1)

            steps(dve, step2, 1, NC + 1)

        @block.tensor
        def _(pe):
            def transpose_x(s):
                pe.wait_ge(xn_ready, 1)
                for kt in range(KT):
                    made = nc.tensor.transpose(xT_bank(s)[:, C * kt:C * kt + C],
                                               xt[s][:, 128 * kt:128 * kt + 128], ident[:, :])
                made.then_inc(xnT_ready[s], 1)

            def transpose_rows(count, count16, b):
                pe.wait_ge(rows_loaded, count16)
                for h in range(2):
                    if count is None:
                        pe.wait_ge((kT_copied[1], p_copied)[h], NC)
                    else:
                        pe.wait_ge(oT_lo_ready[h], count)
                    for j in range(4):
                        c = 128 * (4 * h + j)
                        made = nc.tensor.transpose(TO[h][:, C * j:C * j + C], at_rows[b][:, c:c + 128], ident[:, :])
                    made.then_inc(oT_ready[h], 1)

            def passes(to, parts_T, parts_w, kts, tiles_k):
                hi_T, lo_T = parts_T
                hi_w, lo_w = parts_w
                for kt in kts:
                    for n, (a, w) in enumerate(((hi_T, hi_w), (hi_T, lo_w), (lo_T, hi_w))):
                        made = nc.tensor.matmul(to[:, :], a[:, kt, :], w[:, kt, :], start=(kt == 0 and n == 0),
                                                stop=(kt == tiles_k - 1 and n == 2))
                return made

            def output_product(h, b):
                made = passes(Y[b], (oT_hi, oT_lo), (wo_hi, wo_lo), range(PT // 2 * h, PT // 2 * (h + 1)), PT)
                if h == 1:
                    made.then_inc(Y_ready, 1)

            pe.wait_ge(consts_ready, 1)
            for s in range(2):
                transpose_x(s)

            def step(i, pair, b):
                one = counts(pe, i, 1, (-1, 0, 1))
                pairs = counts(pe, pair, 1, (0, 1))
                start = not exists(i)
                here = exists(i)
                ahead = exists(i + 1)
                wide = b == 1 and ahead
                o = 1 - b

                def product(to, passes, first=0, last=None):
                    last = len(passes) if last is None else last
                    for n in range(first, last):
                        lhs, rhs = passes[n]
                        made = nc.tensor.matmul(to, lhs, rhs, start=(n == 0), stop=(n == len(passes) - 1))
                    return made

                def unit(j, slab_of, ready, first=0, last=None):
                    if start:
                        pe.wait_ge(w_lo_ready, KT * (order.index(slab_of) + 1))
                    made = product(G[j][:, :], [(xp[:, kt, tokens(o)], w[:, slab_of, kt, :]) for kt, xp, w in parts],
                                   first, last)
                    if last is None:
                        made.then_inc(ready, 1)

                parts = [(kt, xp, w) for kt in range(KT)
                         for xp, w in ((xT_hi, w_hi), (xT_hi, w_lo), (xT_lo, w_hi))]

                def k_unit(j):
                    wait(pe, v_ready[j], one[0])
                    unit(j, NP + j, k_unit_ready[j])

                def v_unit(j, first=0, last=None):
                    if wide:
                        pe.wait_ge(exp_q_ready[NQ - 2 + j], pairs[1])
                    else:
                        pe.wait_ge(exp_k_ready[j], one[1])
                    unit(j, 2 * NP + j, v_unit_ready[j], first, last)

                def q_unit(u):
                    if start:
                        pe.wait_ge(w_lo_ready, KT * (order.index(u * QT // KT) + 1))
                    if u == 0:
                        for s in range(2):
                            pe.wait_ge(xT_lo_ready[s], pairs[1])
                    if u < 2:
                        pe.wait_ge(exp_k_ready[u], one[1])
                    else:
                        pe.wait_ge(exp_q_ready[u - 2], pairs[1])
                    for j in range(QT):
                        t = QT * u + j
                        c = 128 * t % U
                        made = product(G[u % 2][:, 2 * C * j:2 * C * j + 2 * C],
                                       [(w[:, 128 * t // U, kt, c:c + 128], xp[:, kt, :]) for kt, xp, w in parts])
                    made.then_inc(q_unit_ready[u], 1)

                def gate_logits():
                    if start:
                        pe.wait_ge(wa_ready, 1)
                    wait(pe, p_copied, one[0])
                    product(z_bank()[0:H, 0:C], [((wa_lo if w is w_lo else wa_hi)[:, kt, :], xp[:, kt, tokens(o)])
                                                 for kt, xp, w in parts]).then_inc(z_ready, 1)

                def transpose_k(j):
                    pe.wait_ge(k_ready[j], one[1])
                    if kT_bank(j, o) is z_bank():
                        pe.wait_ge(exp_z_ready, one[1])
                    elif start:
                        pe.wait_ge(xT_lo_ready[1], 1)
                    elif b == 1:
                        pe.wait_ge(kT_copied[1], one[0])
                    else:
                        pe.wait_ge(p_copied, one[0])
                    for t in range(4):
                        c = U * j + 128 * t
                        made = nc.tensor.transpose(kT_bank(j, o)[:, C * t:C * t + C], k[o][:, c:c + 128], ident[:, :])
                    made.then_inc(kT_ready[j], 1)

                def products():
                    pe.wait_ge(kT_copied[0], one[1])
                    pe.wait_ge(decay_ready, one[1])
                    nc.tensor.matmul(p_bank(o)[:, 0:H], pT[:, :], ident[0:H, 0:H],
                                     start=True, stop=True).then_inc(p_ready, 1)

                def scores(r):
                    if r == 0:
                        for j in range(NP):
                            pe.wait_ge(kT_copied[j], one[0])
                        for u in range(NQ):
                            pe.wait_ge(q_ready[u], pairs[0])
                        wait(pe, M_ready[1], one[-1])
                    else:
                        pe.wait_ge(M_ready[0], one[0])
                    for j in range(2 * GH):
                        two, e = (2 * GH * r + j) // 2, j % 2
                        ps = slice(64 * e, 64 * e + 64)
                        made = nc.tensor.matmul(SC[e][:, C * (j // 2):C * (j // 2) + C], kT[ps, two, :],
                                                qT[ps, two, tokens(b)], start=True, stop=True)
                    made.then_inc(scores_ready[r], 1)

                def group(g):
                    if g == 0:
                        pe.wait_ge(vw_ready, one[0])
                        wait(pe, group_done[NG - 1], one[-1])
                    else:
                        pe.wait_ge(group_done[g - 1], one[0])
                    if g % 2 == 0:
                        pe.wait_ge(M_ready[g // 2], one[0])
                    for j in range(GH):
                        h = GH * g + j
                        nc.tensor.matmul(PV[:, E * j:E * j + E], M[:, h % (2 * GH), :], v1[b][:, h, :],
                                         start=True, stop=True)
                    for j in range(GH):
                        h = GH * g + j
                        c = DELTA + E * (j // 2)
                        nc.tensor.matmul(IN[64 * (h % 2):64 * (h % 2) + 64, c:c + E],
                                                k[b][:, DH * h:DH * h + DH], vw[:, h, :], start=True, stop=True)
                    for j in range(GH // 2):
                        two = GH // 2 * g + j
                        made = nc.tensor.matmul(IN[:, 2 * E * j:2 * E * j + 2 * E], qT[:, two, tokens(b)],
                                         S[:, two, :, :].rearrange("p a e -> p (a e)"), start=True, stop=True)
                    made.then_inc(group_ready[g], 1)

                if ahead:
                    pe.wait_ge(xT_lo_ready[o], pairs[1] if b == 1 else pairs[0])
                    k_unit(0)
                if here:
                    scores(0)
                if ahead:
                    gate_logits()
                    k_unit(1)
                else:
                    pe.wait_ge(wo_lo_ready, KT)
                    for h in range(2):
                        pe.wait_ge(oT_lo_ready[h], 1)
                    pe.wait_ge(v_ready[0], NC)
                    output_product(0, 0)
                if here:
                    group(0)
                if wide:
                    q_unit(0)
                elif ahead:
                    v_unit(0)
                else:
                    scores(1)
                if here:
                    group(1)
                if wide:
                    q_unit(1)
                if here and ahead:
                    scores(1)
                if wide:
                    transpose_k(0)
                    q_unit(2)
                elif ahead:
                    transpose_k(0)
                    transpose_k(1)
                    v_unit(1, 0, 4)
                else:
                    pe.wait_ge(wo_lo_ready, PT)
                    output_product(1, 0)
                if here:
                    group(2)
                if wide:
                    transpose_k(1)
                    products()
                    q_unit(3)
                    if here:
                        group(3)
                    v_unit(0)
                    v_unit(1)
                else:
                    if ahead:
                        v_unit(1, 4)
                        products()
                    if isinstance(i, int) and i == NC - 2:
                        transpose_rows(None, 16, 0)
                    elif not ahead:
                        transpose_rows(1, 32, 1)
                    group(3)

            steps(pe, step, -1, NC)
            pe.wait_ge(v_ready[1], NC)

            def step2(i, _, b):
                one = counts(pe, i, 1, (-2, -1, 0))
                x16 = counts(pe, i, 16, (1,))
                if exists(i):
                    for h in range(2):
                        pe.wait_ge(oT_lo_ready[h], one[0])
                    wait(pe, x1_ready, one[-2])
                    output_product(0, b)
                    if isinstance(i, int) and i == 1:
                        output_product(1, b)
                pe.wait_ge(x1n_ready, one[-1])
                if isinstance(i, int) and i == 1:
                    pe.wait_ge(M_ready[1], NC)
                else:
                    pe.wait_ge(fT_lo_ready, one[-2])
                for j in range(KT):
                    made = nc.tensor.transpose(TF[:, C * j:C * j + C], x1n[1 - b][:, 128 * j:128 * j + 128],
                                               ident[:, :])
                made.then_inc(fT_ready, 1)
                if exists(i) and exists(i - 2):
                    output_product(1, b)
                if exists(i + 1):
                    transpose_rows(one[0], x16[1], 1 - b)
                if isinstance(i, int) and i == 1:
                    pe.wait_ge(wf_lo_ready, KT)
                pe.wait_ge(fT_lo_ready, one[-1])
                if exists(i - 3):
                    pe.wait_ge(y_ready, counts(pe, i, 1, (-3,))[-3])
                else:
                    pe.wait_ge(group_done[NG - 1], NC)
                passes(F[1 - b], (fT_hi, fT_lo), (wf_hi, wf_lo), range(KT), KT).then_inc(F_ready, 1)

            steps(pe, step2, 1, NC + 1)


def kernel(L0_attn_x, L0_attn_Wq, L0_attn_Wk, L0_attn_Wv, L0_attn_Wo, L0_attn_Wa, L0_attn_ba,
           L0_ffn_CB, L0_ffn_SCB, L0_ffn_bias):
    import numpy as np
    import concourse.bacc as bacc
    from concourse.bass_utils import run_bass_kernel_spmd

    pairs = np.asarray(L0_attn_x).reshape(-1, 2 * 128, L0_attn_x.shape[-1])
    ins = dict(x=L0_attn_x, xT=pairs.transpose(0, 2, 1), Wq=L0_attn_Wq, Wk=L0_attn_Wk, Wv=L0_attn_Wv, Wo=L0_attn_Wo, Wa=L0_attn_Wa,
               ba=L0_attn_ba, CBT=np.asarray(L0_ffn_CB).T, SCB=L0_ffn_SCB, bias=L0_ffn_bias)
    nc = bacc.Bacc("TRN2", target_bir_lowering=False, num_devices=1)
    arrays, args = {}, {}
    for name, a in ins.items():
        a = np.ascontiguousarray(a)
        arrays[f"in_{name}"] = a
        args[name] = nc.dram_tensor(f"in_{name}", a.shape, mybir.dt.from_np(a.dtype), kind="ExternalInput").ap()
    shape = arrays["in_x"].shape
    args["out"] = nc.dram_tensor("out_rows", shape, mybir.dt.float32, kind="ExternalOutput").ap()
    gated_linear_attention_block(nc, **args)
    got = run_bass_kernel_spmd(nc, [arrays], core_ids=[0])
    return got.results[0]["out_rows"]
```
